# Optimizing a Trainium2 kernel written in Bass

```python
import numpy as np
import jax
import jax.numpy as jnp

def _softmax(x, axis=-1):
    return jax.nn.softmax(x, axis=axis)

def _gelu(x):
    return jax.nn.gelu(x, approximate=True)

def _silu(x):
    return jax.nn.silu(x)

def _sigmoid(x):
    return jax.nn.sigmoid(x)

def _layernorm(x, axis=-1, eps=1e-05):
    m = jnp.mean(x, axis=axis, keepdims=True)
    v = jnp.var(x, axis=axis, keepdims=True)
    return (x - m) / jnp.sqrt(v + eps)

def _scatter_add(tgt, idx, src, axis=0):
    return tgt.at[idx].add(src)

def _segment_sum(src, seg, n):
    return jax.ops.segment_sum(src, seg, n)
kernel_name = 'mk_seq_postln_d1_jaxref_r8_183fe2'

def setup_inputs(seed: int=0):
    np.random.seed(seed)
    _w = jnp.asarray

    def _L0_attn_setup():
        import jax, jax.numpy as jnp
        from jax import lax
        import numpy as np
        HID = 256
        HK = 8
        HV = 16
        DK = 128
        DV = 128
        KCONV = 4
        KEY_DIM = HK * DK
        VAL_DIM = HV * DV
        CONV_DIM = 2 * KEY_DIM + VAL_DIM
        RMS_EPS = 1e-06
        L2_EPS = 1e-06
        B, S = (2, 128)

        def _l2norm(x, eps=L2_EPS):
            return x * lax.rsqrt(jnp.sum(x * x, axis=-1, keepdims=True) + eps)
        key = jax.random.key(seed)
        ks = jax.random.split(key, 16)

        def w(k, shape, fan_in):
            return jax.random.normal(k, shape, dtype=jnp.float32) * fan_in ** (-0.5)
        return {'hidden_states': jax.random.normal(ks[0], (B, S, HID), dtype=jnp.float32), 'Wqkv': w(ks[1], (CONV_DIM, HID), HID), 'bqkv': jnp.zeros((CONV_DIM,), jnp.float32), 'Wz': w(ks[2], (VAL_DIM, HID), HID), 'bz': jnp.zeros((VAL_DIM,), jnp.float32), 'Wb': w(ks[3], (HV, HID), HID), 'bb': jnp.zeros((HV,), jnp.float32), 'Wa': w(ks[4], (HV, HID), HID), 'ba': jnp.zeros((HV,), jnp.float32), 'conv_w': jax.random.normal(ks[5], (CONV_DIM, KCONV), dtype=jnp.float32) * KCONV ** (-0.5), 'conv_b': jnp.zeros((CONV_DIM,), jnp.float32), 'dt_bias': jnp.ones((HV,), jnp.float32), 'A_log': jnp.log(jax.random.uniform(ks[6], (HV,), jnp.float32, 0.5, 16.0)), 'norm_w': jnp.ones((DV,), jnp.float32), 'Wout': w(ks[7], (HID, VAL_DIM), VAL_DIM), 'bout': jnp.zeros((HID,), jnp.float32)}
    _L0_attn_in = _L0_attn_setup()

    def _L0_ffn_setup():
        import jax, jax.numpy as jnp
        import numpy as np
        NUM_EXPERTS = 64
        TOP_K = 8
        HIDDEN = 256
        INTER = 128
        key = jax.random.key(seed)
        k1, k2, k3, k4 = jax.random.split(key, 4)
        scale = 1.0 / np.sqrt(HIDDEN)
        hidden_states = jax.random.normal(k1, (4, 256, HIDDEN), dtype=jnp.float32)
        gate_w = jax.random.normal(k2, (NUM_EXPERTS, HIDDEN), dtype=jnp.float32) * scale
        w13 = jax.random.normal(k3, (NUM_EXPERTS, 2 * INTER, HIDDEN), dtype=jnp.float32) * scale
        w2 = jax.random.normal(k4, (NUM_EXPERTS, HIDDEN, INTER), dtype=jnp.float32) * (1.0 / np.sqrt(INTER))
        return {'hidden_states': hidden_states, 'gate_w': gate_w, 'w13': w13, 'w2': w2}
    _L0_ffn_in = _L0_ffn_setup()
    _d = {'L0_attn_hidden_states': _L0_attn_in['hidden_states'], 'L0_attn_Wqkv': _L0_attn_in['Wqkv'], 'L0_attn_bqkv': _L0_attn_in['bqkv'], 'L0_attn_Wz': _L0_attn_in['Wz'], 'L0_attn_bz': _L0_attn_in['bz'], 'L0_attn_Wb': _L0_attn_in['Wb'], 'L0_attn_bb': _L0_attn_in['bb'], 'L0_attn_Wa': _L0_attn_in['Wa'], 'L0_attn_ba': _L0_attn_in['ba'], 'L0_attn_conv_w': _L0_attn_in['conv_w'], 'L0_attn_conv_b': _L0_attn_in['conv_b'], 'L0_attn_dt_bias': _L0_attn_in['dt_bias'], 'L0_attn_A_log': _L0_attn_in['A_log'], 'L0_attn_norm_w': _L0_attn_in['norm_w'], 'L0_attn_Wout': _L0_attn_in['Wout'], 'L0_attn_bout': _L0_attn_in['bout'], 'L0_ffn_gate_w': _L0_ffn_in['gate_w'], 'L0_ffn_w13': _L0_ffn_in['w13'], 'L0_ffn_w2': _L0_ffn_in['w2']}
    _x0 = _d['L0_attn_hidden_states']
    _d['L0_attn_hidden_states'] = jax.random.normal(jax.random.fold_in(jax.random.key(seed), 1), (8, 256, 256), dtype=_x0.dtype)
    del _x0
    return _d

def reference(L0_attn_hidden_states, L0_attn_Wqkv, L0_attn_bqkv, L0_attn_Wz, L0_attn_bz, L0_attn_Wb, L0_attn_bb, L0_attn_Wa, L0_attn_ba, L0_attn_conv_w, L0_attn_conv_b, L0_attn_dt_bias, L0_attn_A_log, L0_attn_norm_w, L0_attn_Wout, L0_attn_bout, L0_ffn_gate_w, L0_ffn_w13, L0_ffn_w2):

    def _L0_attn_ref(hidden_states, Wqkv, bqkv, Wz, bz, Wb, bb, Wa, ba, conv_w, conv_b, dt_bias, A_log, norm_w, Wout, bout):
        import jax, jax.numpy as jnp
        from jax import lax
        import numpy as np
        HID = 256
        HK = 8
        HV = 16
        DK = 128
        DV = 128
        KCONV = 4
        KEY_DIM = HK * DK
        VAL_DIM = HV * DV
        CONV_DIM = 2 * KEY_DIM + VAL_DIM
        RMS_EPS = 1e-06
        L2_EPS = 1e-06
        B, S = (2, 128)

        def _l2norm(x, eps=L2_EPS):
            return x * lax.rsqrt(jnp.sum(x * x, axis=-1, keepdims=True) + eps)
        b, s, _ = hidden_states.shape
        mixed = hidden_states @ Wqkv.T + bqkv
        z = hidden_states @ Wz.T + bz
        beta = jax.nn.sigmoid(hidden_states @ Wb.T + bb)
        a = hidden_states @ Wa.T + ba
        g = -jnp.exp(A_log) * jax.nn.softplus(a + dt_bias)
        x = mixed.transpose(0, 2, 1)
        y = lax.conv_general_dilated(x, conv_w[:, None, :], (1,), [(KCONV - 1, 0)], dimension_numbers=('NCH', 'OIH', 'NCH'), feature_group_count=CONV_DIM) + conv_b[None, :, None]
        mixed = jax.nn.silu(y).transpose(0, 2, 1)
        q = mixed[..., :KEY_DIM].reshape(b, s, HK, DK)
        k = mixed[..., KEY_DIM:2 * KEY_DIM].reshape(b, s, HK, DK)
        v = mixed[..., 2 * KEY_DIM:].reshape(b, s, HV, DV)
        rep = HV // HK
        q = jnp.repeat(q, rep, axis=2)
        k = jnp.repeat(k, rep, axis=2)
        q = _l2norm(q) * DK ** (-0.5)
        k = _l2norm(k)
        qt = q.transpose(1, 0, 2, 3)
        kt = k.transpose(1, 0, 2, 3)
        vt = v.transpose(1, 0, 2, 3)
        gt = g.transpose(1, 0, 2)
        bt = beta.transpose(1, 0, 2)
        state0 = jnp.zeros((b, HV, DK, DV), jnp.float32)

        def step(state, inp):
            q_t, k_t, v_t, g_t, b_t = inp
            state = state * jnp.exp(g_t)[..., None, None]
            kv_mem = jnp.einsum('bhk,bhkv->bhv', k_t, state)
            delta = (v_t - kv_mem) * b_t[..., None]
            state = state + k_t[..., None] * delta[:, :, None, :]
            out = jnp.einsum('bhk,bhkv->bhv', q_t, state)
            return (state, out)
        _, outs = lax.scan(step, state0, (qt, kt, vt, gt, bt))
        core = outs.transpose(1, 0, 2, 3)
        zg = z.reshape(b, s, HV, DV)
        var = jnp.mean(core * core, axis=-1, keepdims=True)
        core = core * lax.rsqrt(var + RMS_EPS) * norm_w * jax.nn.silu(zg)
        core = core.reshape(b, s, VAL_DIM)
        return core @ Wout.T + bout

    def _L0_ffn_ref(hidden_states, gate_w, w13, w2):
        import jax, jax.numpy as jnp
        import numpy as np
        NUM_EXPERTS = 64
        TOP_K = 8
        HIDDEN = 256
        INTER = 128
        orig_shape = hidden_states.shape
        x = hidden_states.reshape(-1, HIDDEN)
        logits = jnp.einsum('th,eh->te', x, gate_w)
        probs = jax.nn.softmax(logits, axis=-1)
        topk_w, topk_idx = jax.lax.top_k(probs, TOP_K)
        combine = (jax.nn.one_hot(topk_idx, NUM_EXPERTS, dtype=x.dtype) * topk_w[..., None]).sum(axis=1)

        def step(acc, inp):
            w13_e, w2_e, c = inp
            g = x @ w13_e[:INTER].T
            u = x @ w13_e[INTER:].T
            h = jax.nn.silu(g) * u
            o = h @ w2_e.T
            return (acc + c[:, None] * o, None)
        out0 = jnp.zeros_like(x)
        out, _ = jax.lax.scan(step, out0, (w13, w2, combine.T))
        return out.reshape(orig_shape)
    x = L0_attn_hidden_states
    x = _layernorm(x + _L0_attn_ref(x, L0_attn_Wqkv, L0_attn_bqkv, L0_attn_Wz, L0_attn_bz, L0_attn_Wb, L0_attn_bb, L0_attn_Wa, L0_attn_ba, L0_attn_conv_w, L0_attn_conv_b, L0_attn_dt_bias, L0_attn_A_log, L0_attn_norm_w, L0_attn_Wout, L0_attn_bout), axis=-1)
    x = _layernorm(x + _L0_ffn_ref(x, L0_ffn_gate_w, L0_ffn_w13, L0_ffn_w2), axis=-1)
    return x

_drawn_inputs = setup_inputs


def setup_inputs(seed=0):
    import zlib

    import numpy as np

    out = dict(_drawn_inputs(seed))
    spreads = {'L0_attn_bqkv': (0.0, 0.1),
     'L0_attn_bz': (0.0, 0.1),
     'L0_attn_bb': (0.0, 0.684),
     'L0_attn_ba': (0.0, 0.8),
     'L0_attn_conv_b': (0.0, 0.1),
     'L0_attn_dt_bias': (1.0, 0.6),
     'L0_attn_norm_w': (1.0, 0.2),
     'L0_attn_bout': (0.0, 0.1)}
    factors = {}
    for name, (base, spread) in spreads.items():
        noise = np.random.default_rng([zlib.crc32(name.encode()), seed]).standard_normal(out[name].shape)
        drawn = base * np.exp(spread * noise) if base else spread * noise
        out[name] = jnp.asarray(drawn.astype(out[name].dtype))
    for name, factor in factors.items():
        out[name] = (out[name] * factor).astype(out[name].dtype)
    return out
```

```python
from contextlib import ExitStack

import concourse.bass as bass
from concourse import mybir

F32 = mybir.dt.float32
I32 = mybir.dt.int32
U32 = mybir.dt.uint32
ALU = mybir.AluOpType
ACT = mybir.ActivationFunctionType

P = 128
HID = 256
KC = HID // P
NB, SEQ = 8, 256
TOK = NB * SEQ
NT = TOK // P
HK, HV = 8, 16
REP = HV // HK
PAIRS = NB // 2
ST = 2 * SEQ
TPS = ST // P
KCONV = 4
LEVELS = 6
Q32 = 32
PACKED = 4
L2_EPS = 1e-6
RMS_EPS = 1e-6
LN_EPS = 1e-5
V0, V1, K_, Q_ = range(4)
NPRM = 6
F_G, F_BETA, F_EG, F_NEG, F_DEC = range(5)
NF = 5

C_ID, C_UINC, C_LSTR, C_KKQ, C_B32, C_L32, C_LEV = 0, 128, 256, 384, 640, 768, 896
C_I32 = C_LEV + (PACKED + 1) * Q32
C_TAU = C_I32 + Q32
NCONST = C_TAU + 2

NE, TOPK, INTER = 64, 8, 128
XT_TILES = (TOK * TOPK + NE * (P - 1)) // P + 1
SLOTS = XT_TILES * P
WCOL = KC * 2 * INTER + HID
U = 4
XTURNS = XT_TILES // U
assert XT_TILES % U == 0 and XT_TILES <= 2 * P
ZROWS = 4


class Sig:

    def __init__(self, handle, per_step, steps):
        self.handle, self.per_step, self.steps = handle, per_step, steps

    def value(self, it, i):
        turn, step = it
        return turn * (self.steps * self.per_step) + (step * self.per_step + i)


def wait(eng, sig, it, i):
    v = sig.value(it, i)
    if isinstance(v, int) and v <= 0:
        return
    eng.wait_ge(sig.handle, v)


def attention(nc, cst, acc, zeros, x_t, x_n, w_v, w_kq, w_z, prm, w_ab, rows, w_out, norm_w, consts, xs):
    with ExitStack() as ctx:
        def sb(name, *shape, dt=F32):
            return ctx.enter_context(nc.sbuf_tensor(name, [P, *shape], dt))[:]

        def bank(name):
            return ctx.enter_context(nc.psum_tensor(name, [P, 512], F32))[:]

        def sem(name):
            return ctx.enter_context(nc.semaphore(name))

        def sig(name, per_step):
            return Sig(sem(name), per_step, PAIRS)

        xT = sb("xT", KC, TOK)
        wo = sb("wo", HV, HID)
        wab = sb("wab", KC, 2 * HV)
        rowb = sb("rowb", 4 * HV + HID)
        nw = sb("nw", 1)
        ones = sb("ones", 1)
        gates = sb("gates", HK, NF * 2 * NT)
        wv = sb("wv", KC, 2 * P)
        wkq = sb("wkq", KC, 2 * P)
        wz = sb("wz", KC, 2 * P)
        pv_ = sb("pv", 2 * NPRM)
        pkq = sb("pkq", 2 * NPRM)
        pz = sb("pz", 2)
        kq = [sb(f"kq{i}", TPS, 2, P) for i in range(2)]
        vT = [sb(f"vT{i}", 2, ST) for i in range(2)]
        zT = [sb(f"zT{i}", 2, ST) for i in range(2)]
        sc = [sb(f"sc{i}", NF, 2 * TPS) for i in range(2)]
        b2 = [sb(f"b2{i}", 2 * TPS) for i in range(2)]
        epsq = [sb(f"epsq{i}", TPS) for i in range(2)]
        irt = [sb(f"irt{i}", TPS) for i in range(2)]
        PT = [sb(f"PT{i}", 2, 4, P) for i in range(2)]
        raw = [sb(f"raw{i}", 2, KCONV - 1 + SEQ) for i in range(2)]
        yc = [sb(f"yc{i}", 2, SEQ) for i in range(2)]
        th = [sb(f"th{i}", ST) for i in range(2)]
        zr = [sb(f"zr{i}", ST) for i in range(2)]
        zth = [sb(f"zth{i}", ST) for i in range(2)]
        ksq = sb("ksq", TPS, 2, P)
        kss_k = sb("kss_k", TPS)
        kss_h = sb("kss_h", TPS)
        rcp = sb("rcp", TPS)
        ms = sb("ms", 2 * 4)
        msb = sb("msb", 2 * 4)
        rO = sb("rO", 2 * 4)
        expo = sb("expo", 2, 8)
        gm = sb("gm", 2, 4, P)
        E = sb("E", 2, 4, P)
        kkqm = sb("kkqm", 2, 2, 2, P)
        LT = sb("LT", 2, 4, P)
        LTD = sb("LTD", 2, 4, P)
        LT4 = sb("LT4", 2, 4, P)
        Xp = sb("Xp", 2, 4, Q32)
        XTp = sb("XTp", 2, 4, Q32)
        XT = sb("XT", 2, 4, P)
        T1p = sb("T1p", 2, 4, Q32)
        T1F = sb("T1F", 2, 4, P)
        X64 = sb("X64", 2, 4, 64)
        T15 = sb("T15", 2, 4, 64)
        XTF = sb("XTF", 2, 4, P)
        vn = sb("vn", 2, 4, P)
        kn = sb("kn", 2, P)
        dl = sb("dl", 2, 4, P)
        dec = sb("dec", 2, 2, P)
        ssb = sb("ssb", 2, 2 * P)
        w1 = sb("w1", 2, 2, P)
        qse = sb("qse", 2, 2, P)
        osb = sb("osb", 2, 4, P)
        osc = sb("osc", 2, 4, P)
        gT = sb("gT", 2, 4, P)

        SB = [bank(f"solve{g}") for g in range(2)]
        PB = [bank(f"proj{i}") for i in range(2)]
        A = [bank(f"tailA{g}") for g in range(2)]
        B = [bank(f"tailB{g}") for g in range(2)]

        in_const, in_x, in_acc, in_misc, in_wo = (sem(n) for n in ("in_const", "in_x", "in_acc", "in_misc", "in_wo"))
        in_wv, in_wkq, in_wz = sem("in_wv"), sem("in_wkq"), sem("in_wz")
        set_pool, set_dve, set_act, set_pe = sem("set_pool"), sem("set_dve"), sem("set_act"), sem("set_pe")
        kkq, diff = sig("kkq", 2), sig("diff", 2)
        t1, xu = sig("t1", 2 * LEVELS), sig("xu", 2 * LEVELS)
        d0, s0, ksqs, d1, o_, ot, wo_ = (sig(n, 2) for n in ("d0", "s0", "ksqs", "d1", "o", "ot", "wo_d"))
        proj, zproj, kss = sig("proj", 4), sig("zproj", 2), sig("kss", 1)
        vt, knt = sig("vt", 2), sig("knt", 2)
        exp_, dl0, ssev, rawd, tap3, tanh = sig("exp", 2), sig("dl0", 2), sig("ssev", 2), sig("raw_d", 4), sig("tap3", 4), sig("tanh", 4)
        zraw, ztanh, qsed, dl1 = sig("zraw", 2), sig("ztanh", 2), sig("qse_d", 2), sig("dl1", 2)
        xeA, ltdA, t1a, xtc, x64a = sig("xeA", PACKED + 1), sig("ltdA", 1), sig("t1a", 4), sig("xtc", 2), sig("x64a", 2)
        sqd, vnd, knd, ksqd = sig("sqd", 2), sig("vnd", 2), sig("knd", 2), sig("ksqd", 1)
        kkqd, kssd, rcpd, b2d, decd, ltd, xp0 = sig("kkqd", 2), sig("kssd", 1), sig("rcpd", 1), sig("b2d", 1), sig("decd", 2), sig("ltd", 2), sig("xp0", 4)
        xd, xtpd, t1d, offd, xtfd = sig("xd", 2 * PACKED + 2), sig("xtpd", 2 * PACKED + 2), sig("t1d", 2 * PACKED), sig("offd", 4), sig("xtfd", 2)
        taps, silu, zsilu = sig("taps", 12), sig("silu", 4), sig("zsilu", 2)
        w1d, osbd, msd, oscd, gtd, accd, scd = sig("w1d", 2), sig("osbd", 2), sig("msd", 1), sig("oscd", 2), sig("gtd", 2), sig("accd", 2), sig("scd", 1)
        irtd, ptd, rOd, gmd = sig("irtd", 1), sig("ptd", 2), sig("rOd", 1), sig("gmd", 2)
        ltdP, lt4d, xeP = sig("ltdP", 1), sig("lt4d", 2), sig("xeP", PACKED + 1)
        zeroed = sem("zeroed")
        of_set_up = [t.rearrange("p g a t -> p (g a t)")[:, n * NT * HV:(n + 1) * NT * HV].rearrange("p (t h) -> p t h", h=HV)
                     for t, n in ((osb, 0), (osb, 1), (osb, 2), (osb, 3), (gT, 0), (gT, 1))]
        ga, gb, gab, ge, gl, gg = of_set_up
        rowa = sb("rowa", HV)
        eal = sb("eal", HV)

        ident = cst[:, C_ID:C_ID + P]
        uinc = cst[:, C_UINC:C_UINC + P]
        lstr = cst[:, C_LSTR:C_LSTR + P]

        def rep4(c):
            return cst[:, c:c + P].unsqueeze(1).to_broadcast([P, 4, P])

        def rep_packed(c):
            return cst[:, c:c + Q32].unsqueeze(1).to_broadcast([P, 4, Q32])

        def quad(t, g, b, n=1, cols=None):
            t = t[b * Q32:(b + n) * Q32, g]
            return t if cols is None else t[:, :, cols * Q32:(cols + n) * Q32]

        def packed_psum(g, i, b=0, n=4):
            return SB[g][b * Q32:(b + n) * Q32, i * P:(i + 1) * P].rearrange("p (a t) -> p a t", a=4)

        def prm_of(c):
            t = (pv_ if c in (V0, V1) else pkq)[:, (c % 2) * NPRM:(c % 2 + 1) * NPRM]
            return t

        def col(t, i):
            return t[:, i:i + 1]

        def dst_of(c, p):
            if c in (V0, V1):
                return vT[p][:, c, :].rearrange("p (n t) -> p n t", t=P)
            return kq[p][:, :, c - K_, :]

        def g_col(p, f, g, v, c):
            i = (2 * g + c) * 2 + v
            return sc[p][:, f, i:i + 1]

        def b2_col(p, g, v, c):
            i = (2 * g + c) * 2 + v
            return b2[p][:, i:i + 1]

        block = ctx.enter_context(nc.Block())
        LAST = (HK - 1, PAIRS - 1)

        def run_steps(eng, step):
            for pair in range(PAIRS):
                step((0, pair), first=pair == 0, last=False)
            with eng.Fori(1, HK - 1) as hk:
                for pair in range(PAIRS):
                    step((hk, pair), first=False, last=False)
            for pair in range(PAIRS):
                step((HK - 1, pair), first=False, last=pair == PAIRS - 1)

        @block.sync
        def _(sp):
            sp.dma_start(cst, consts).then_inc(in_const, 16)
            sp.dma_start(xT, x_t).then_inc(in_x, 16)
            for s, t in ((w_ab, wab), (rows, rowb), (norm_w, nw)):
                sp.dma_start(t, s).then_inc(in_misc, 16)

            def load_head(hk, part):
                if part == 0:
                    sp.dma_start(wv, w_v[bass.ds(hk, 1)].rearrange("a p k n -> p (a k) n")).then_inc(in_wv, 16)
                    sp.dma_start(pv_, prm[bass.ds(hk, 1), :, 0:12].rearrange("a p n -> p (a n)")).then_inc(in_wv, 16)
                elif part == 1:
                    sp.dma_start(wkq, w_kq[bass.ds(hk, 1)].rearrange("a p k n -> p (a k) n")).then_inc(in_wkq, 16)
                    sp.dma_start(pkq, prm[bass.ds(hk, 1), :, 12:24].rearrange("a p n -> p (a n)")).then_inc(in_wkq, 16)
                else:
                    sp.dma_start(wz, w_z[bass.ds(hk, 1)].rearrange("a p k n -> p (a k) n")).then_inc(in_wz, 16)
                    sp.dma_start(pz, prm[bass.ds(hk, 1), :, 24:26].rearrange("a p n -> p (a n)")).then_inc(in_wz, 16)

            for part in range(3):
                load_head(0, part)
            sp.dma_start(wo, w_out).then_inc(in_wo, 16)
            sp.dma_start(acc, x_n).then_inc(in_acc, 16)
            sp.wait_ge(set_pool, 1)
            for n in range(SLOTS // (P * ZROWS)):
                sp.dma_start(xs[n * P * ZROWS:(n + 1) * P * ZROWS, :].rearrange("(p a) n -> p (a n)", p=P), zeros).then_inc(zeroed, 16)
            with sp.Fori(0, HK - 1) as hk:
                wait(sp, silu, (hk, PAIRS - 1), 2)
                load_head(hk + 1, 0)
                wait(sp, silu, (hk, PAIRS - 1), 4)
                load_head(hk + 1, 1)
                wait(sp, zraw, (hk, PAIRS - 1), 2)
                load_head(hk + 1, 2)
            sp.wait_ge(zeroed, 16 * (SLOTS // (P * ZROWS)))

        @block.tensor
        def _(pe):
            mm = nc.tensor.matmul

            def project(nx, c, parts=range(KC)):
                w_ = wv if c in (V0, V1) else wkq
                for k in parts:
                    last = mm(PB[c % 2], w_[:, k, (c % 2) * P:(c % 2 + 1) * P],
                              xT[:, k, (nx[1] % PAIRS) * ST:(nx[1] % PAIRS + 1) * ST], start=k == 0, stop=k == KC - 1)
                if KC - 1 in parts:
                    last.then_inc(proj.handle, 1)

            def products(nx, p):
                for g in range(2):
                    wait(pe, silu, nx, 4)
                    wait(pe, zraw, (nx[0], nx[1] - 1), g + 1)
                    for c in range(2):
                        tile = kq[p][:, 2 * g + c, :, :]
                        m = mm(PB[g][:, c * 256:(c + 1) * 256], tile[:, 0, :], tile.rearrange("p a t -> p (a t)"), start=True, stop=True)
                    m.then_inc(kkq.handle, 1)

            def head_of(nx):
                return nx[0] + nx[1] // PAIRS

            def weights_in(s, hk):
                pe.wait_ge(s, hk * 32 + 32)

            def tail_d0(pv):
                for g in range(2):
                    wait(pe, vnd, pv, g + 1)
                    wait(pe, xtfd, pv, g + 1)
                    for v in range(2):
                        m = mm(A[g][:, v * P:(v + 1) * P], XTF[:, g, 2 * v, :], vn[:, g, 2 * v, :], start=True, stop=True)
                    m.then_inc(d0.handle, 1)

            def tail_s0(pv):
                for g in range(2):
                    wait(pe, decd, pv, g + 1)
                    wait(pe, knd, pv, g + 1)
                    mm(B[g][:, 0:256], kn[:, g, :], dec[:, g].rearrange("p a t -> p (a t)"), start=True, stop=True).then_inc(s0.handle, 1)

            def tail_ksqs(pv, q):
                for g in range(2):
                    wait(pe, ssev, pv, g + 1)
                    rhs = ssb[:, g, :]
                    mm(A[g][:, 256:512], kq[q][:, 2 * g + 1, 0, :], rhs, start=True, stop=True)
                    mm(B[g][:, 256:512], kq[q][:, 2 * g + 1, 1, :], rhs, start=True, stop=True).then_inc(ksqs.handle, 1)

            def tail_d1(pv):
                for g in range(2):
                    wait(pe, w1d, pv, g + 1)
                    for v in range(2):
                        m = mm(A[g][:, v * P:(v + 1) * P], XTF[:, g, 2 * v + 1, :], w1[:, g, v, :], start=True, stop=True)
                    m.then_inc(d1.handle, 1)

            def tail_o(pv, q):
                for g in range(2):
                    wait(pe, dl1, pv, g + 1)
                    wait(pe, qsed, pv, g + 1)
                    for i in range(4):
                        m = mm(B[g][:, i * P:(i + 1) * P], PT[q][:, g, i, :], dl[:, g, i, :], start=True, stop=True)
                    m.then_inc(o_.handle, 1)

            def tail_ot(pv):
                for g in range(2):
                    wait(pe, oscd, pv, g + 1)
                    for i in range(4):
                        m = nc.tensor.transpose(A[g][:, i * P:(i + 1) * P], osc[:, g, i, :], ident)
                    m.then_inc(ot.handle, 1)

            def tail_wo(pv):
                hk = pv[0] + pv[1] // PAIRS
                for g in range(2):
                    wait(pe, gtd, pv, g + 1)
                    for c in range(2):
                        for v in range(2):
                            m = mm(B[g][:, c * 256:(c + 1) * 256], gT[:, g, 2 * v + c, :],
                                   wo.rearrange("p h n -> p (h n)")[:, bass.ds((hk * REP + v) * HID, HID)], start=v == 0, stop=v == 1)
                    m.then_inc(wo_.handle, 1)

            def step(it, first, last):
                hk, pair = it
                p, q = pair % 2, 1 - pair % 2
                nx, pv = (hk, pair + 1), (hk, pair - 1)
                xs = slice(pair * ST, (pair + 1) * ST)
                tail = not first

                wait(pe, ksqd, it, 1)
                wait(pe, kkqd, it, 2)
                for i in range(2 * TPS):
                    mmi = mm(PB[0][:, i:i + 1], ksq[:, i // 2, i % 2, :], ones, start=True, stop=True)
                mmi.then_inc(kss.handle, 1)
                for g in range(2):
                    wait(pe, gmd, it, g + 1)
                    wait(pe, xtfd, pv, g + 1)
                    mm(SB[g], lstr, gm[:, g].rearrange("p a t -> p (a t)"), start=True, stop=True).then_inc(diff.handle, 1)
                if tail:
                    tail_d0(pv)

                def level_t1(l):
                    for g in range(2):
                        if l == 0:
                            wait(pe, (ltdP, ltdA)[g], it, 1)
                        if l < PACKED:
                            wait(pe, xd, it, 2 * l + g + 1)
                        elif l == PACKED:
                            wait(pe, xd, it, 2 * l + g + 1)
                            wait(pe, lt4d, it, g + 1)
                        else:
                            wait(pe, offd, it, 2 + g + 1)
                            wait(pe, x64a, it, g + 1)
                        for i in range(4):
                            if l <= PACKED:
                                m = mm(SB[g][:, i * Q32:(i + 1) * Q32], (LTD if l < PACKED else LT4)[:, g, i, :], Xp[:, g, i, :], start=True, stop=True)
                            else:
                                m = mm(SB[g][:, i * 64:(i + 1) * 64], LT[0:64, g, i, :], X64[0:64, g, i, :], start=True, stop=True)
                        m.then_inc(t1.handle, 1)

                def level_xu(l):
                    for g in range(2):
                        if l < PACKED:
                            wait(pe, t1d, it, 2 * l + g + 1)
                            wait(pe, (xeP, xeA)[g], it, l + 1)
                            for i in range(4):
                                m = mm(SB[g][:, P + i * Q32:P + (i + 1) * Q32], XT[:, g, i, :], T1p[:, g, i, :], start=True, stop=True)
                        elif l == PACKED:
                            wait(pe, t1a, it, g + 1)
                            wait(pe, xtpd, it, 2 * PACKED + g + 1)
                            for i in range(4):
                                m = mm(SB[g][:, P + i * Q32:P + (i + 1) * Q32], T1F[:, g, i, :], XTp[:, g, i, :], start=True, stop=True)
                        else:
                            wait(pe, t1a, it, 2 + g + 1)
                            for i in range(4):
                                m = mm(SB[g][0:64, 256 + i * 64:256 + (i + 1) * 64], T15[:, g, i, :], XTF[:, g, i, 64:128], start=True, stop=True)
                        m.then_inc(xu.handle, 1)

                def project_z(v, parts):
                    for k in parts:
                        m = mm(PB[v], wz[:, k, v * P:(v + 1) * P], xT[:, k, xs], start=k == 0, stop=k == KC - 1)
                    if KC - 1 in parts:
                        m.then_inc(zproj.handle, 1)

                if not last:
                    weights_in(in_wv, head_of(nx))
                    wait(pe, kssd, it, 1)
                    project(nx, V0)
                if tail:
                    tail_s0(pv)
                if not last:
                    project(nx, V1)
                if tail:
                    tail_ksqs(pv, q)
                level_t1(0)
                if tail:
                    tail_d1(pv)
                level_xu(0)
                if not last:
                    weights_in(in_wkq, head_of(nx))
                    wait(pe, rawd, nx, V0 + 1)
                    project(nx, K_)
                level_t1(1)
                if tail:
                    tail_o(pv, q)
                level_xu(1)
                if not last:
                    wait(pe, rawd, nx, V1 + 1)
                    project(nx, Q_)
                level_t1(2)
                weights_in(in_wz, hk)
                if not last:
                    wait(pe, rawd, nx, K_ + 1)
                else:
                    wait(pe, kssd, it, 1)
                project_z(0, [0])
                level_xu(2)
                project_z(0, [1])
                level_t1(3)
                if not last:
                    wait(pe, rawd, nx, Q_ + 1)
                project_z(1, [0])
                level_xu(3)
                project_z(1, [1])
                if tail:
                    tail_ot(pv)
                level_t1(4)
                level_xu(4)
                if tail:
                    tail_wo(pv)
                level_t1(5)
                for g in range(2):
                    for v in range(2):
                        for c in range(2):
                            t = 2 * g + c
                            m = nc.tensor.transpose(A[g][:, (2 * v + c) * P:(2 * v + c + 1) * P], vT[p][:, v, t * P:(t + 1) * P], ident)
                    m.then_inc(vt.handle, 1)
                if not last:
                    products(nx, q)
                for g in range(2):
                    if tail:
                        wait(pe, accd, pv, g + 1)
                    nc.tensor.transpose(B[g][:, 0:P], kq[p][:, 2 * g, 0, :], ident).then_inc(knt.handle, 1)
                level_xu(5)

            def final_tail():
                q = LAST[1] % 2
                tail_d0(LAST)
                tail_s0(LAST)
                tail_ksqs(LAST, q)
                tail_d1(LAST)
                tail_o(LAST, q)
                tail_ot(LAST)
                tail_wo(LAST)

            pe.wait_ge(in_x, 16)
            pe.wait_ge(in_misc, 48)
            for t in range(NT):
                for k in range(KC):
                    m = mm(SB[0][:, t * 32:(t + 1) * 32], xT[:, k, t * P:(t + 1) * P], wab[:, k, :], start=k == 0, stop=k == KC - 1)
            m.then_inc(set_pe, 1)
            pe.wait_ge(in_const, 16)
            pe.wait_ge(set_dve, 5)
            mm(A[0][:, 0:256], uinc, gg.rearrange("p t h -> p (t h)"), start=True, stop=True)
            mm(A[1][:, 0:256], lstr, gg.rearrange("p t h -> p (t h)"), start=True, stop=True).then_inc(set_pe, 1)
            for c in range(4):
                weights_in(in_wv if c in (V0, V1) else in_wkq, 0)
                if c >= 2:
                    wait(pe, rawd, (0, 0), c - 1)
                project((0, 0), c)
            pe.wait_ge(set_act, 5)
            products((0, 0), 0)
            run_steps(pe, step)
            final_tail()

        @block.scalar
        def _(act):
            av = nc.scalar.activation

            def conv_in(nx, c):
                pr = prm_of(c)
                wait(act, proj, nx, c + 1)
                wait(act, taps, nx, 3 * (c - 1))
                av(raw[c % 2][:, :, KCONV - 1:], PB[c % 2].rearrange("p (b t) -> p b t", b=2), ACT.Identity, bias=col(pr, 0)).then_inc(rawd.handle, 1)
                wait(act, silu, nx, c - 1)
                wait(act, rawd, nx, c + 1)
                av(yc[c % 2], raw[c % 2][:, :, KCONV - 1:], ACT.Identity, bias=col(pr, 1), scale=col(pr, 5)).then_inc(tap3.handle, 1)

            def conv_tanh(nx, c):
                wait(act, taps, nx, 3 * (c + 1))
                av(th[c % 2], yc[c % 2].rearrange("p b t -> p (b t)"), ACT.Tanh, scale=0.5).then_inc(tanh.handle, 1)

            def z_in(it, v):
                wait(act, zproj, it, v + 1)
                wait(act, zsilu, it, v - 1)
                av(zr[v], PB[v], ACT.Identity, bias=col(pz, v)).then_inc(zraw.handle, 1)
                wait(act, zraw, it, v + 1)
                av(zth[v], zr[v], ACT.Tanh, scale=0.5).then_inc(ztanh.handle, 1)

            def ltd_out(it):
                wait(act, ltd, it, 2)
                for b in range(4):
                    a = av(quad(LTD, 1, b, cols=b), quad(LT, 1, b, cols=b), ACT.Copy)
                a.then_inc(ltdA.handle, 1)

            def xt_expand(it, l):
                wait(act, xtpd, it, 2 * l + 2)
                for b in range(4):
                    a = av(quad(XT, 1, b, cols=b), quad(XTp, 1, b), ACT.Copy)
                a.then_inc(xeA.handle, 1)

            def t1_out4(it):
                for g in range(2):
                    wait(act, t1, it, 2 * PACKED + g + 1)
                    for b in (1, 3):
                        a = av(quad(T1F, g, b, cols=b - 1), packed_psum(g, 0, b, 1), ACT.Copy)
                    a.then_inc(t1a.handle, 1)

            def x64_out(it):
                for g in range(2):
                    wait(act, (xeP, xeA)[g], it, PACKED + 1)
                    av(XTF[:, g], XT[:, g], ACT.Copy).then_inc(xtc.handle, 1)
                    for b in (0, 1):
                        a = av(quad(X64, g, b, cols=b), quad(Xp, g, b), ACT.Copy)
                    a.then_inc(x64a.handle, 1)

            def t1_out5(it):
                for g in range(2):
                    wait(act, t1, it, 2 * LEVELS - 2 + g + 1)
                    av(T15[64:128, g], SB[g][64:128, 0:256].rearrange("p (a t) -> p a t", a=4), ACT.Copy).then_inc(t1a.handle, 1)

            def square(nx, p):
                wait(act, silu, nx, 4)
                av(ksq, kq[p], ACT.Square).then_inc(ksqd.handle, 1)

            def t_dl0(pv, q):
                for g in range(2):
                    wait(act, d0, pv, g + 1)
                    for v in range(2):
                        a = av(dl[:, g, 2 * v, :], A[g][:, v * P:(v + 1) * P], ACT.Copy, scale=b2_col(q, g, v, 0))
                    a.then_inc(dl0.handle, 1)

            def t_dec(pv, q):
                for g in range(2):
                    wait(act, dl0, pv, g + 1)
                    for v in range(2):
                        a = av(dec[:, g, v, :], dl[:, g, 2 * v, :], ACT.Copy, scale=g_col(q, F_DEC, g, v, 0))
                    a.then_inc(decd.handle, 1)

            def t_state(pv):
                for g in range(2):
                    wait(act, s0, pv, g + 1)
                    av(ssb[:, g, :], B[g][:, 0:256], ACT.Copy).then_inc(ssev.handle, 1)

            def t_qse(pv, q):
                for g in range(2):
                    wait(act, ksqs, pv, g + 1)
                    for v in range(2):
                        a = av(qse[:, g, v, :], B[g][:, 256 + v * P:256 + (v + 1) * P], ACT.Copy, scale=g_col(q, F_EG, g, v, 1))
                    a.then_inc(qsed.handle, 1)

            def t_dl1(pv, q):
                for g in range(2):
                    wait(act, d1, pv, g + 1)
                    for v in range(2):
                        a = av(dl[:, g, 2 * v + 1, :], A[g][:, v * P:(v + 1) * P], ACT.Copy, scale=b2_col(q, g, v, 1))
                    a.then_inc(dl1.handle, 1)

            def t_square(pv):
                for g in range(2):
                    wait(act, osbd, pv, g + 1)
                    for i in range(4):
                        a = av(osc[:, g, i, :], osb[:, g, i, :], ACT.Square, accum_out=ms[:, 4 * g + i:4 * g + i + 1])
                    a.then_inc(sqd.handle, 1)

            def step(it, first, last):
                hk, pair = it
                p, q = pair % 2, 1 - pair % 2
                nx, pv = (hk, pair + 1), (hk, pair - 1)
                tail = not first
                for g in range(2):
                    wait(act, diff, it, g + 1)
                    wait(act, ptd, pv, g + 1)
                    av(E[:, g].rearrange("p a t -> p (a t)"), SB[g], ACT.Exp).then_inc(exp_.handle, 1)
                if tail:
                    t_dl0(pv, q)
                    t_dec(pv, q)
                if not last:
                    if pair == PAIRS - 1:
                        act.wait_ge(in_wv, (hk + 1) * 32 + 32)
                    conv_in(nx, V0)
                if tail:
                    t_state(pv)
                ltd_out(it)
                if tail:
                    t_qse(pv, q)
                xt_expand(it, 0)
                if not last:
                    conv_tanh(nx, V0)
                    conv_in(nx, V1)
                if tail:
                    t_dl1(pv, q)
                xt_expand(it, 1)
                if not last:
                    if pair == PAIRS - 1:
                        act.wait_ge(in_wkq, (hk + 1) * 32 + 32)
                    conv_in(nx, K_)
                    conv_tanh(nx, V1)
                xt_expand(it, 2)
                if tail:
                    t_square(pv)
                if not last:
                    conv_tanh(nx, K_)
                    conv_in(nx, Q_)
                xt_expand(it, 3)
                if pair == 0:
                    act.wait_ge(in_wz, hk * 32 + 32)
                z_in(it, 0)
                if not last:
                    conv_tanh(nx, Q_)
                z_in(it, 1)
                t1_out4(it)
                xt_expand(it, 4)
                x64_out(it)
                t1_out5(it)
                if not last:
                    square(nx, q)
                for g in range(2):
                    wait(act, vt, it, g + 1)
                    wait(act, irtd, it, 1)
                    for v in range(2):
                        for c in range(2):
                            t = 2 * g + c
                            a = av(vn[:, g, 2 * v + c, :], A[g][:, (2 * v + c) * P:(2 * v + c + 1) * P], ACT.Copy, scale=irt[p][:, t:t + 1])
                    a.then_inc(vnd.handle, 1)
                for g in range(2):
                    wait(act, knt, it, g + 1)
                    av(kn[:, g, :], B[g][:, 0:P], ACT.Copy).then_inc(knd.handle, 1)

            act.wait_ge(set_dve, 2)
            act.wait_ge(in_misc, 48)
            av(ge, gab, ACT.Exp, scale=-1.0)
            av(eal, rowb[:, 3 * HV:4 * HV], ACT.Exp).then_inc(set_act, 1)
            act.wait_ge(set_act, 1)
            av(gl, ge, ACT.Ln, bias=1.0).then_inc(set_act, 1)
            act.wait_ge(set_dve, 3)
            av(gb, gb, ACT.Tanh, scale=0.5).then_inc(set_act, 1)

            def field(f):
                return gates.rearrange("p h (f t v) -> p h f t v", f=NF, v=2)[:, :, f]

            def by_head(t):
                return t.rearrange("p t (h v) -> p h t v", v=2)

            act.wait_ge(set_pe, 2)
            for h in range(HK):
                av(field(F_EG)[:, h], A[0][:, 0:256].rearrange("p (t h v) -> p h t v", h=HK, v=2)[:, h], ACT.Exp)
                a = av(field(F_DEC)[:, h], A[1][:, 0:256].rearrange("p (t h v) -> p h t v", h=HK, v=2)[:, h], ACT.Exp)
            a.then_inc(set_act, 2)
            act.wait_ge(in_wv, 32)
            act.wait_ge(in_wkq, 32)
            for c in range(4):
                conv_in((0, 0), c)
                conv_tanh((0, 0), c)
            square((0, 0), 0)
            run_steps(act, step)
            t_dl0(LAST, 1)
            t_dec(LAST, 1)
            t_state(LAST)
            t_qse(LAST, 1)
            t_dl1(LAST, 1)
            t_square(LAST)

        @block.vector
        def _(dve):
            tt, stt, ts = nc.vector.tensor_tensor, nc.vector.scalar_tensor_tensor, nc.vector.tensor_scalar

            def conv_taps(nx, c):
                pr = prm_of(c)
                y = yc[c % 2]
                wait(dve, rawd, nx, c + 1)
                wait(dve, tap3, nx, c + 1)
                for j in range(KCONV - 1):
                    if j:
                        wait(dve, taps, nx, 3 * c + j)
                    stt(y, raw[c % 2][:, :, j:j + SEQ], col(pr, 2 + j), y, ALU.mult, ALU.add).then_inc(taps.handle, 1)

            def conv_silu(nx, c, p):
                wait(dve, tanh, nx, c + 1)
                stt(dst_of(c, p), th[c % 2].rearrange("p (n t) -> p n t", t=P), 1.0,
                    yc[c % 2].rearrange("p b (n t) -> p (b n) t", t=P), ALU.add, ALU.mult).then_inc(silu.handle, 1)

            def z_silu(it, v, p):
                wait(dve, ztanh, it, v + 1)
                stt(zT[p][:, v, :], zth[v], 1.0, zr[v], ALU.add, ALU.mult).then_inc(zsilu.handle, 1)

            def gates_of(nx, p):
                hk, pair = nx[0] + nx[1] // PAIRS, nx[1] % PAIRS
                src = gates.rearrange("p h (f t) -> p h f t", f=NF)[:, bass.ds(hk, 1), :, pair * 2 * TPS:(pair + 1) * 2 * TPS]
                tt(sc[p], src.rearrange("p h f t -> p (h f) t"), src.rearrange("p h f t -> p (h f) t"), ALU.max).then_inc(scd.handle, 1)

            def t1_out(it, l):
                for g in range(2):
                    wait(dve, t1, it, 2 * l + g + 1)
                    tt(T1p[:, g], packed_psum(g, 0), rep_packed(C_LEV + (l + 1) * Q32), ALU.mult).then_inc(t1d.handle, 1)

            def x_start(it):
                for g in range(2):
                    wait(dve, ltd, it, g + 1)
                    for b in range(4):
                        a = nc.vector.transpose(quad(Xp, g, b), quad(LT, g, b, cols=b))
                    a.then_inc(xp0.handle, 1)
                for g in range(2):
                    wait(dve, xp0, it, g + 1)
                    tt(Xp[:, g], Xp[:, g], rep_packed(C_LEV), ALU.mult).then_inc(xp0.handle, 1)
                for g in range(2):
                    wait(dve, xp0, it, 2 + g + 1)
                    tt(Xp[:, g], rep_packed(C_I32), Xp[:, g], ALU.subtract).then_inc(xd.handle, 1)

            def xtp_out(it, l):
                for g in range(2):
                    wait(dve, xd, it, 2 * l + g + 1)
                    nc.vector.transpose(XTp[:, g], Xp[:, g]).then_inc(xtpd.handle, 1)

            def x_out(it, l):
                for g in range(2):
                    wait(dve, xu, it, 2 * l + g + 1)
                    tt(Xp[:, g], Xp[:, g], packed_psum(g, 1), ALU.subtract).then_inc(xd.handle, 1)
                xtp_out(it, l + 1)

            def x_out4(it):
                for g in range(2):
                    wait(dve, xu, it, 2 * PACKED + g + 1)
                    wait(dve, xtc, it, g + 1)
                    for b in (0, 2):
                        a = ts(quad(XTF, g, b)[:, :, (b + 1) * Q32:(b + 2) * Q32], packed_psum(g, 1, b, 1), -1.0, None, ALU.mult)
                    a.then_inc(offd.handle, 1)
                for g in range(2):
                    wait(dve, offd, it, g + 1)
                    nc.vector.transpose(quad(X64, g, 1, cols=0), quad(XTF, g, 0, cols=1)).then_inc(offd.handle, 1)

            def x_out5(it):
                for g in range(2):
                    wait(dve, xu, it, 2 * LEVELS - 2 + g + 1)
                    ts(XTF[0:64, g, :, 64:128], SB[g][0:64, 256:512].rearrange("p (a t) -> p a t", a=4), -1.0, None, ALU.mult).then_inc(xtfd.handle, 1)

            def products_out(nx):
                for g in range(2):
                    wait(dve, kkq, nx, g + 1)
                    wait(dve, ptd, (nx[0], nx[1] - 1), g + 1)
                    tt(kkqm[:, g].rearrange("p c a t -> p c (a t)"), PB[g].rearrange("p (c n) -> p c n", c=2),
                       cst[:, C_KKQ:C_KKQ + 256].unsqueeze(1).to_broadcast([P, 2, 256]), ALU.mult).then_inc(kkqd.handle, 1)

            def t_w1(pv, q):
                for g in range(2):
                    wait(dve, ksqs, pv, g + 1)
                    for v in range(2):
                        a = stt(w1[:, g, v, :], A[g][:, 256 + v * P:256 + (v + 1) * P], g_col(q, F_NEG, g, v, 1), vn[:, g, 2 * v + 1, :], ALU.mult, ALU.add)
                    a.then_inc(w1d.handle, 1)

            def t_osb(pv):
                for g in range(2):
                    wait(dve, o_, pv, g + 1)
                    wait(dve, qsed, pv, g + 1)
                    ov = osb[:, g].rearrange("p (v c) t -> p v c t", v=2)
                    bv = B[g].rearrange("p (v c t) -> p v c t", v=2, c=2)
                    nc.vector.tensor_copy(ov[:, :, 0], bv[:, :, 0])
                    tt(ov[:, :, 1], bv[:, :, 1], qse[:, g], ALU.add).then_inc(osbd.handle, 1)

            def t_ms(pv, q):
                wait(dve, sqd, pv, 2)
                ep = epsq[q].rearrange("p (g c) -> p g c", g=2)
                for g in range(2):
                    a = stt(msb[:, 4 * g:4 * g + 4].rearrange("p (v c) -> p v c", v=2), ms[:, 4 * g:4 * g + 4].rearrange("p (v c) -> p v c", v=2),
                            4.0 / P, ep[:, g].unsqueeze(1).to_broadcast([P, 2, 2]), ALU.mult, ALU.add)
                a.then_inc(msd.handle, 1)

            def t_gate(pv, q):
                for g in range(2):
                    wait(dve, ot, pv, g + 1)
                    tt(gT[:, g].rearrange("p (v c) t -> p v (c t)", v=2), A[g].rearrange("p (v n) -> p v n", v=2),
                       zT[q][:, :, g * SEQ:(g + 1) * SEQ], ALU.mult).then_inc(gtd.handle, 1)

            def t_acc(pv):
                pr = pv[1] % PAIRS
                for g in range(2):
                    wait(dve, wo_, pv, g + 1)
                    a_ = acc[:, pr * TPS + 2 * g:pr * TPS + 2 * g + 2, :]
                    tt(a_, a_, B[g].rearrange("p (c n) -> p c n", c=2), ALU.add).then_inc(accd.handle, 1)

            def step(it, first, last):
                hk, pair = it
                p, q = pair % 2, 1 - pair % 2
                nx, pv = (hk, pair + 1), (hk, pair - 1)
                tail = not first
                wait(dve, kss, it, 1)
                ksv = PB[0][:, 0:2 * TPS].rearrange("p (t a) -> p a t", a=2)
                ts(kss_k, ksv[:, 0], 4 * L2_EPS, None, ALU.add)
                ts(kss_h, ksv[:, 0], 4 * L2_EPS, 0.25, ALU.add, ALU.mult)
                ts(epsq[p], ksv[:, 1], 4 * L2_EPS, 4 * RMS_EPS * P, ALU.add, ALU.mult).then_inc(kssd.handle, 1)
                wait(dve, kssd, it, 1)
                nc.vector.reciprocal(rcp, kss_k).then_inc(rcpd.handle, 1)
                wait(dve, rcpd, it, 1)
                tt(b2[p].rearrange("p (t v) -> p t v", v=2), sc[p][:, F_BETA].rearrange("p (t v) -> p t v", v=2),
                   rcp.unsqueeze(2).to_broadcast([P, TPS, 2]), ALU.mult).then_inc(b2d.handle, 1)
                wait(dve, b2d, it, 1)
                for g in range(2):
                    wait(dve, exp_, it, g + 1)
                    for v in range(2):
                        for c in range(2):
                            a = stt(LT[:, g, 2 * v + c, :], kkqm[:, g, c, 0, :], b2_col(p, g, v, c), E[:, g, 2 * v + c, :], ALU.mult, ALU.mult)
                    a.then_inc(ltd.handle, 1)
                x_start(it)
                xtp_out(it, 0)
                if tail:
                    t_w1(pv, q)
                t1_out(it, 0)
                if not last:
                    conv_taps(nx, V0)
                x_out(it, 0)
                t1_out(it, 1)
                if not last:
                    conv_silu(nx, V0, q)
                    conv_taps(nx, V1)
                x_out(it, 1)
                if tail:
                    t_osb(pv)
                if not last:
                    conv_silu(nx, V1, q)
                t1_out(it, 2)
                if not last:
                    conv_taps(nx, K_)
                x_out(it, 2)
                if tail:
                    t_ms(pv, q)
                if not last:
                    conv_silu(nx, K_, q)
                t1_out(it, 3)
                if not last:
                    conv_taps(nx, Q_)
                    gates_of(nx, q)
                x_out(it, 3)
                z_silu(it, 0, p)
                if tail:
                    t_gate(pv, q)
                if not last:
                    conv_silu(nx, Q_, q)
                x_out4(it)
                z_silu(it, 1, p)
                if tail:
                    t_acc(pv)
                if not last:
                    products_out(nx)
                x_out5(it)

            nc.vector.memset(ones, 1.0)
            nc.vector.memset(zeros, 0.0)
            for z_ in (LTD, XT, T1F, X64, T15):
                nc.vector.memset(z_, 0.0)
            nc.vector.memset(expo[:, 0, :], 0.5)
            nc.vector.memset(expo[:, 1, :], -0.5)
            for i in range(2):
                a = nc.vector.memset(raw[i][:, :, 0:KCONV - 1], 0.0)
            a.then_inc(set_pool, 1)
            dve.wait_ge(in_misc, 48)
            tt(rowa, rowb[:, HV:2 * HV], rowb[:, 2 * HV:3 * HV], ALU.add).then_inc(set_dve, 1)
            dve.wait_ge(set_dve, 1)
            dve.wait_ge(set_pe, 1)
            abv = SB[0].rearrange("p (t n) -> p t n", t=NT)

            def rows_of(r):
                return r.unsqueeze(1).to_broadcast([P, NT, HV])

            tt(gb, abv[:, :, 0:HV], rows_of(rowb[:, 0:HV]), ALU.add)
            tt(ga, abv[:, :, HV:2 * HV], rows_of(rowa), ALU.add).then_inc(set_pool, 1)
            dve.wait_ge(set_pool, 2)
            stt(gab, ga, -1.0, ga, ALU.mult, ALU.max).then_inc(set_dve, 1)
            ts(ga, ga, 0.0, None, ALU.max).then_inc(set_dve, 1)
            dve.wait_ge(set_act, 2)
            dve.wait_ge(set_dve, 3)
            tt(gl, gl, ga, ALU.add).then_inc(set_dve, 1)
            dve.wait_ge(set_dve, 4)
            stt(gg, gl, -1.0, rows_of(eal), ALU.mult, ALU.mult).then_inc(set_dve, 1)
            dve.wait_ge(set_dve, 5)
            dve.wait_ge(set_act, 5)
            gf = gates.rearrange("p h (f t v) -> p h f t v", f=NF, v=2)
            for h in range(HK):
                hv = slice(2 * h, 2 * h + 2)
                nc.vector.tensor_copy(gf[:, h, F_G], gg[:, :, hv])
                ts(gf[:, h, F_BETA], gb[:, :, hv], 0.5, 0.5, ALU.mult, ALU.add)
                a = ts(gf[:, h, F_NEG], gf[:, h, F_EG], -1.0, None, ALU.mult)
            a.then_inc(set_dve, 1)
            dve.wait_ge(set_dve, 6)
            gates_of((0, 0), 0)
            for c in range(4):
                if c in (V0, K_):
                    dve.wait_ge(in_wv if c == V0 else in_wkq, 32)
                conv_taps((0, 0), c)
                conv_silu((0, 0), c, 0)
            dve.wait_ge(in_wo, 16)
            ts(wo, wo, nw, None, ALU.mult)
            dve.wait_ge(in_acc, 16)
            tt(acc, acc, rowb[:, 4 * HV:].unsqueeze(1).to_broadcast([P, NT, HID]), ALU.add).then_inc(set_dve, 1)
            dve.wait_ge(set_dve, 7)
            wait(dve, scd, (0, 0), 1)
            products_out((0, 0))
            run_steps(dve, step)
            t_w1(LAST, 1)
            t_osb(LAST)
            t_ms(LAST, 1)
            t_gate(LAST, 1)
            t_acc(LAST)

        @block.gpsimd
        def _(pool):
            pt_ = nc.gpsimd.tensor_tensor

            def decay_rows(nx, p):
                wait(pool, scd, nx, 1)
                for g in range(2):
                    wait(pool, diff, nx, g + 1 - 2)
                    src = sc[p][:, F_G, 4 * g:4 * g + 4].rearrange("p (c v) -> p v c", v=2)
                    pt_(gm[:, g].rearrange("p (v c) t -> p v c t", v=2),
                        uinc.unsqueeze(1).unsqueeze(1).to_broadcast([P, 2, 2, P]),
                        src.unsqueeze(3).to_broadcast([P, 2, 2, P]), ALU.mult).then_inc(gmd.handle, 1)

            def t_root(pv):
                wait(pool, msd, pv, 1)
                pt_(rO, msb, expo[:, 1, :], ALU.pow).then_inc(rOd.handle, 1)

            def t_scale(pv):
                wait(pool, rOd, pv, 1)
                for g in range(2):
                    pt_(osc[:, g], osb[:, g], rO[:, 4 * g:4 * g + 4].unsqueeze(2).to_broadcast([P, 4, P]), ALU.mult).then_inc(oscd.handle, 1)

            def step(it, first, last):
                hk, pair = it
                p, q = pair % 2, 1 - pair % 2
                nx, pv = (hk, pair + 1), (hk, pair - 1)
                wait(pool, kssd, it, 1)
                pt_(irt[p], kss_h, expo[:, 0, 0:TPS], ALU.pow).then_inc(irtd.handle, 1)
                wait(pool, ltd, it, 1)
                pt_(LTD[:, 0], LT[:, 0], rep4(C_B32), ALU.mult).then_inc(ltdP.handle, 1)

                def expand(l):
                    wait(pool, xtpd, it, 2 * l + 1)
                    pt_(XT[:, 0].rearrange("p a (b t) -> p a b t", t=Q32), XTp[:, 0].unsqueeze(2).to_broadcast([P, 4, P // Q32, Q32]),
                        rep4(C_B32).rearrange("p a (b t) -> p a b t", t=Q32), ALU.mult).then_inc(xeP.handle, 1)

                expand(0)
                wait(pool, ltd, it, 2)
                for g in range(2):
                    pt_(LT4[:, g], LT[:, g], rep4(C_L32), ALU.mult).then_inc(lt4d.handle, 1)
                expand(1)
                for g in range(2):
                    wait(pool, exp_, it, g + 1)
                    kv = kkqm[:, g, :, 1, :].unsqueeze(1).to_broadcast([P, 2, 2, P])
                    pt_(PT[p][:, g].rearrange("p (v c) t -> p v c t", v=2), E[:, g].rearrange("p (v c) t -> p v c t", v=2), kv, ALU.mult).then_inc(ptd.handle, 1)
                expand(2)
                expand(3)
                if not first:
                    t_root(pv)
                    t_scale(pv)
                expand(4)
                if not last:
                    decay_rows(nx, q)

            pool.wait_ge(in_const, 16)
            pool.wait_ge(set_pool, 1)
            decay_rows((0, 0), 0)
            run_steps(pool, step)
            t_root(LAST)
            t_scale(LAST)


def experts(nc, cst, acc, gate_t, w_e, xs, ys, out):
    with ExitStack() as ctx:
        def sb(name, *shape, dt=F32, parts=P):
            return ctx.enter_context(nc.sbuf_tensor(name, [parts, *shape], dt))[:]

        def bank(name):
            return ctx.enter_context(nc.psum_tensor(name, [P, 512], F32))[:]

        def sem(name):
            return ctx.enter_context(nc.semaphore(name))

        def sig(name):
            return Sig(sem(name), 1, U)

        ident = cst[:, C_ID:C_ID + P]
        before = cst[:, C_KKQ:C_KKQ + P]
        stats, mv, veps, rstd = sb("stats", NT, 6), sb("mv", NT, 2), sb("veps", NT), sb("rstd", NT)
        half = sb("half", NT)
        gw = sb("gw", KC, NE)
        x1T = [sb(f"x1T{i}", KC, P) for i in range(2)]
        probs, picked = sb("probs", NT, NE), sb("picked", NT, NE)
        mx, rs = sb("mx", NT), sb("rs", NT)
        v8 = sb("v8", NT, TOPK)
        prior = sb("prior", NT + 1, NE)
        allones = sb("allones", P)
        cnt_i, tiles_i = sb("cnt_i", NE, dt=I32), sb("tiles_i", NE, dt=I32)
        tiles, cum, base, base1 = sb("tiles", NE), sb("cum", NE), sb("base", NE), sb("base1", NE)
        pos, p8 = sb("pos", NT, NE), sb("p8", NT, TOPK)
        idx = sb("idx", NT, TOPK, dt=I32)
        cmp_ = sb("cmp", 2, NE)
        ec = sb("ec", 2)
        eid = sb("eid", 2 * P, dt=I32, parts=1)
        eq = sb("eq", NT, NE)
        eqp = sb("eqp", NT, NE)
        wj = sb("wj", TOPK, NT)
        we = [sb(f"we{i}", WCOL) for i in range(U)]
        xr = [sb(f"xr{i}", HID) for i in range(U)]
        yr = [sb(f"yr{i}", HID) for i in range(U)]
        xeT = [sb(f"xeT{i}", KC * P) for i in range(2)]
        sg = [sb(f"sg{i}", P) for i in range(2)]
        hT = [sb(f"hT{i}", P) for i in range(2)]
        gath = [sb(f"gath{i}", TOPK, HID) for i in range(2)]
        PS = [bank(f"ps{i}") for i in range(8)]
        RT, LB, PF = PS[0:2], PS[2:4], PS[4:6]
        CB, EB = PS[6], PS[7]

        in_gw, ln_stats, ln_var, ln_r, x1d = (sem(n) for n in ("in_gw", "ln_stats", "ln_var", "ln_r", "x1d"))
        rt, rte, lg, mxd, sub, ex, sm, rsd, prd, v8d, repd, pick = (
            sem(n) for n in ("rt", "rte", "lg", "mxd", "sub", "ex", "sm", "rsd", "prd", "v8d", "repd", "pick"))
        prid, pfd, cntd, tl, cumd, bsd, posd, p8d, idxd, cmpd, ecd, ebd, eidd, scat, ones_d = (
            sem(n) for n in ("prid", "pfd", "cntd", "tl", "cumd", "bsd", "posd", "p8d", "idxd", "cmpd", "ecd", "ebd", "eidd", "scat", "ones_d"))

        eqd, wjd = sem("eqd"), sem("wjd")
        x_in, w_in, y_out_d = ([sem(f"{n}{u}") for u in range(U)] for n in ("x_in", "w_in", "y_st"))
        trd, xtd, gud, sgd, hd, w2d, yd = (sig(n) for n in ("trd", "xtd", "gud", "sgd", "hd", "w2d", "yd"))
        g_in = [sem(f"g_in{i}") for i in range(2)]
        summed, fin_stats, fin_var, fin_r, fin_x, out_sem = (sem(n) for n in ("summed", "fin_stats", "fin_var", "fin_r", "fin_x", "out_sem"))

        with nc.Block() as block:
            @block.sync
            def _(sp):
                sp.dma_start(gw, gate_t).then_inc(in_gw, 16)

            @block.gpsimd
            def _(pool):
                pool.wait_ge(ln_r, 1)
                nc.gpsimd.tensor_tensor(rstd, veps, half, ALU.pow).then_inc(ln_r, 1)
                pool.wait_ge(idxd, 1)
                for t in range(NT):
                    for j in range(TOPK):
                        nc.gpsimd.indirect_dma_start(out=xs, out_offset=bass.IndirectOffsetOnAxis(idx[:, t, j:j + 1].bitcast(U32), 0),
                                                     in_=acc[:, t, :], in_offset=None).then_inc(scat, 16)
                pool.wait_ge(scat, 16 * NT * TOPK)

            @block.scalar
            def _(act):
                for t in range(NT):
                    act.wait_ge(rt, t + 1)
                    if t >= 2:
                        act.wait_ge(lg, t - 1)
                    nc.scalar.activation(x1T[t % 2].rearrange("p k t -> p (k t)"), RT[t % 2][:, 0:KC * P], ACT.Copy).then_inc(rte, 1)
                act.wait_ge(sub, 2)
                nc.scalar.activation(picked, probs, ACT.Exp).then_inc(ex, 1)

            @block.tensor
            def _(pe):
                pe.wait_ge(in_gw, 16)

                def logits(t):
                    pe.wait_ge(rte, t + 1)
                    for k in range(KC):
                        m = nc.tensor.matmul(LB[t // 8][:, (t % 8) * NE:(t % 8 + 1) * NE], x1T[t % 2][:, k, :], gw[:, k, :], start=k == 0, stop=k == KC - 1)
                    m.then_inc(lg, 1)

                for t in range(NT):
                    pe.wait_ge(x1d, t + 1)
                    if t >= 2:
                        pe.wait_ge(rte, t - 1)
                    for k in range(KC):
                        m = nc.tensor.transpose(RT[t % 2][:, k * P:(k + 1) * P], acc[:, t, k * P:(k + 1) * P], ident)
                    m.then_inc(rt, 1)
                    if t:
                        logits(t - 1)
                logits(NT - 1)
                pe.wait_ge(pick, 1)
                pe.wait_ge(prid, NT)
                for i in range(2):
                    nc.tensor.matmul(PF[i], before, picked[:, 8 * i:8 * i + 8, :].rearrange("p t e -> p (t e)"), start=True, stop=False)
                    nc.tensor.matmul(PF[i], allones, prior[:, 8 * i:8 * i + 8, :].rearrange("p t e -> p (t e)"), start=False, stop=True).then_inc(pfd, 1)
                nc.tensor.matmul(CB[:, 0:NE], allones, prior[:, NT, :], start=True, stop=True).then_inc(cntd, 1)
                pe.wait_ge(ecd, 2)
                for i in range(2):
                    m = nc.tensor.transpose(EB[0:1, i * P:(i + 1) * P], ec[:, i:i + 1], ident)
                m.then_inc(ebd, 1)

            @block.vector
            def _(dve):
                tt, stt, ts = nc.vector.tensor_tensor, nc.vector.scalar_tensor_tensor, nc.vector.tensor_scalar
                nc.vector.memset(half, -0.5)
                nc.vector.memset(prior[:, 0, :], 0.0)
                nc.vector.memset(allones, 1.0).then_inc(ones_d, 1)
                for t in range(NT):
                    nc.vector.bn_stats(stats[:, t, :], acc[:, t, :]).then_inc(ln_stats, 1)
                for t in range(NT):
                    dve.wait_ge(ln_stats, t + 1)
                    nc.vector.bn_aggr(mv[:, t, :], stats[:, t, :]).then_inc(ln_var, 1)
                dve.wait_ge(ln_var, NT)
                ts(veps, mv[:, :, 1], LN_EPS, None, ALU.add).then_inc(ln_r, 1)
                dve.wait_ge(ln_r, 2)
                for t in range(NT):
                    ts(acc[:, t, :], acc[:, t, :], mv[:, t, 0:1], rstd[:, t:t + 1], ALU.subtract, ALU.mult).then_inc(x1d, 1)
                dve.wait_ge(lg, NT)
                lv = [b.rearrange("p (t e) -> p t e", e=NE) for b in LB]
                for i in range(2):
                    nc.vector.reduce_max(mx[:, 8 * i:8 * i + 8], lv[i], mybir.AxisListType.X).then_inc(mxd, 1)
                for i in range(2):
                    dve.wait_ge(mxd, i + 1)
                    tt(probs[:, 8 * i:8 * i + 8, :], lv[i], mx[:, 8 * i:8 * i + 8].unsqueeze(2).to_broadcast([P, 8, NE]), ALU.subtract).then_inc(sub, 1)
                dve.wait_ge(ex, 1)
                nc.vector.reduce_sum(mx, picked, mybir.AxisListType.X).then_inc(sm, 1)
                dve.wait_ge(sm, 1)
                nc.vector.reciprocal(rs, mx).then_inc(rsd, 1)
                dve.wait_ge(rsd, 1)
                tt(probs, picked, rs.unsqueeze(2).to_broadcast([P, NT, NE]), ALU.mult).then_inc(prd, 1)
                dve.wait_ge(prd, 1)
                for t in range(NT):
                    nc.vector.max(v8[:, t, :], probs[:, t, :]).then_inc(v8d, 1)
                for t in range(NT):
                    dve.wait_ge(v8d, t + 1)
                    nc.vector.match_replace(eq[:, t, :], v8[:, t, :], probs[:, t, :], -1.0).then_inc(repd, 1)
                dve.wait_ge(repd, NT)
                ts(picked, eq, 0.0, None, ALU.is_lt).then_inc(pick, 1)
                dve.wait_ge(pick, 1)
                for t in range(NT):
                    if t:
                        dve.wait_ge(prid, t)
                    tt(prior[:, t + 1, :], prior[:, t, :], picked[:, t, :], ALU.add).then_inc(prid, 1)
                dve.wait_ge(cntd, 1)
                ts(cnt_i, CB[:, 0:NE], float(P - 1), None, ALU.add).then_inc(tl, 1)
                dve.wait_ge(tl, 1)
                ts(tiles_i, cnt_i, P.bit_length() - 1, None, ALU.logical_shift_right).then_inc(tl, 1)
                dve.wait_ge(tl, 2)
                nc.vector.tensor_copy(tiles, tiles_i).then_inc(tl, 1)
                dve.wait_ge(tl, 3)
                nc.vector.tensor_tensor_scan(cum, allones[:, 0:NE], tiles, 0.0, ALU.mult, ALU.add).then_inc(cumd, 1)
                dve.wait_ge(cumd, 1)
                tt(base, cum, tiles, ALU.subtract).then_inc(bsd, 1)
                tt(cmp_, cum.unsqueeze(1).to_broadcast([P, 2, NE]), cst[:, C_TAU:C_TAU + 2].unsqueeze(2).to_broadcast([P, 2, NE]), ALU.is_le).then_inc(cmpd, 1)
                dve.wait_ge(bsd, 1)
                ts(base1, base, float(P), 1.0, ALU.mult, ALU.add).then_inc(bsd, 1)
                dve.wait_ge(cmpd, 1)
                nc.vector.reduce_sum(ec, cmp_, mybir.AxisListType.X).then_inc(ecd, 1)
                dve.wait_ge(ecd, 1)
                ts(ec, ec, float(NE - 1), None, ALU.min).then_inc(ecd, 1)
                dve.wait_ge(pfd, 2)
                dve.wait_ge(bsd, 2)
                for i in range(2):
                    tt(pos[:, 8 * i:8 * i + 8, :], PF[i].rearrange("p (t e) -> p t e", e=NE), base1.unsqueeze(1).to_broadcast([P, 8, NE]), ALU.add).then_inc(posd, 1)
                dve.wait_ge(posd, 2)
                tt(pos, pos, picked, ALU.mult).then_inc(posd, 1)
                dve.wait_ge(posd, 3)
                for t in range(NT):
                    nc.vector.max(p8[:, t, :], pos[:, t, :]).then_inc(p8d, 1)
                dve.wait_ge(p8d, NT)
                ts(idx, p8, 1.0, None, ALU.subtract).then_inc(idxd, 1)
                dve.wait_ge(ebd, 1)
                nc.vector.tensor_copy(eid, EB[0:1, 0:2 * P]).then_inc(eidd, 1)
                dve.wait_ge(eidd, 1)
                for j in range(TOPK):
                    if j:
                        dve.wait_ge(wjd, j)
                    tt(eq, pos, p8[:, :, j:j + 1].to_broadcast([P, NT, NE]), ALU.is_equal).then_inc(eqd, 1)
                    dve.wait_ge(eqd, 2 * j + 1)
                    tt(eqp, eq, probs, ALU.mult).then_inc(eqd, 1)
                    dve.wait_ge(eqd, 2 * j + 2)
                    nc.vector.reduce_sum(wj[:, j, :], eqp, mybir.AxisListType.X).then_inc(wjd, 1)

        with nc.Block() as block:
            def run_turns(eng, step):
                for u in range(U):
                    step((0, u), first=u == 0, last=False)
                with eng.Fori(1, XTURNS - 1) as turn:
                    for u in range(U):
                        step((turn, u), first=False, last=False)
                for u in range(U):
                    step((XTURNS - 1, u), first=False, last=u == U - 1)

            @block.sync
            def _(sp):
                def step(it, first, last):
                    turn, u = it
                    tile = turn * U + u
                    wait(sp, w2d, (turn, u - U), 1)
                    e = sp.value_load(eid[0:1, bass.ds(tile, 1)], min_val=0, max_val=NE - 1)
                    sp.dma_start(xr[u], xs[bass.ds(tile * P, P), :]).then_inc(x_in[u], 16)
                    sp.dma_start(we[u], w_e[bass.ds(e, 1)].rearrange("a p n -> p (a n)")).then_inc(w_in[u], 16)

                run_turns(sp, step)

            @block.tensor
            def _(pe):
                def turn_x(tile, i):
                    turn, u = tile
                    pe.wait_ge(x_in[u % U], (turn + u // U) * 16 + 16)
                    for k in range(KC):
                        m = nc.tensor.transpose(PS[u % 2][:, k * P:(k + 1) * P], xr[u % U][:, k * P:(k + 1) * P], ident)
                    m.then_inc(trd.handle, 1)

                def down(tile):
                    turn, u = tile
                    wait(pe, hd, tile, 1)
                    wait(pe, yd, (turn, u - 2), 1)
                    nc.tensor.matmul(PS[4 + u % 2][:, 0:HID], hT[u % 2], we[u % U][:, KC * 2 * INTER:], start=True, stop=True).then_inc(w2d.handle, 1)

                def step(it, first, last):
                    turn, u = it
                    if not last:
                        turn_x((turn, u + 1), 0)
                    pe.wait_ge(w_in[u], turn * 16 + 16)
                    wait(pe, xtd, it, 1)
                    wait(pe, hd, (turn, u - 2), 1)
                    for f in range(2):
                        for k in range(KC):
                            m = nc.tensor.matmul(PS[2 + u % 2][:, f * P:(f + 1) * P], we[u][:, (2 * k + f) * P:(2 * k + f + 1) * P],
                                                 xeT[u % 2][:, k * P:(k + 1) * P], start=k == 0, stop=k == KC - 1)
                    m.then_inc(gud.handle, 1)
                    if not first:
                        down((turn, u - 1))

                turn_x((0, 0), 0)
                run_turns(pe, step)
                down((XTURNS - 1, U - 1))

            @block.scalar
            def _(act):
                def y_out(tile):
                    turn, u = tile
                    wait(act, w2d, tile, 1)
                    if u % U or True:
                        n = (turn + (u - U) // U) * 16 + 16
                        if not (isinstance(n, int) and n <= 0):
                            act.wait_ge(y_out_d[u % U], n)
                    nc.scalar.activation(yr[u % U], PS[4 + u % 2][:, 0:HID], ACT.Copy).then_inc(yd.handle, 1)
                    wait(act, yd, tile, 1)
                    act.dma_start(ys[bass.ds((turn * U + u) * P, P), :], yr[u % U]).then_inc(y_out_d[u % U], 16)

                def step(it, first, last):
                    turn, u = it
                    wait(act, gud, it, 1)
                    nc.scalar.activation(sg[u % 2], PS[2 + u % 2][:, 0:P], ACT.Silu).then_inc(sgd.handle, 1)
                    if not first:
                        y_out((turn, u - 1))

                run_turns(act, step)
                y_out((XTURNS - 1, U - 1))
                for u in range(U):
                    act.wait_ge(y_out_d[u], 16 * XTURNS)

            @block.vector
            def _(dve):
                def h_out(tile):
                    turn, u = tile
                    wait(dve, sgd, tile, 1)
                    nc.vector.tensor_tensor(hT[u % 2], sg[u % 2], PS[2 + u % 2][:, P:2 * P], ALU.mult).then_inc(hd.handle, 1)

                def x_out(tile):
                    turn, u = tile
                    wait(dve, trd, tile, 1)
                    nc.vector.tensor_copy(xeT[u % 2], PS[u % 2][:, 0:KC * P]).then_inc(xtd.handle, 1)

                def step(it, first, last):
                    turn, u = it
                    if not last:
                        x_out((turn, u + 1))
                    h_out(it)

                x_out((0, 0))
                run_turns(dve, step)

        with nc.Block() as block:
            @block.gpsimd
            def _(pool):
                for t in range(NT):
                    if t >= 2:
                        pool.wait_ge(summed, TOPK * (t - 1))
                    for j in range(TOPK):
                        nc.gpsimd.indirect_dma_start(out=gath[t % 2][:, j, :], out_offset=None, in_=ys,
                                                     in_offset=bass.IndirectOffsetOnAxis(idx[:, t, j:j + 1].bitcast(U32), 0)).then_inc(g_in[t % 2], 16)
                pool.wait_ge(fin_r, 1)
                nc.gpsimd.tensor_tensor(rstd, veps, half, ALU.pow).then_inc(fin_r, 1)

            @block.vector
            def _(dve):
                ts = nc.vector.tensor_scalar
                for t in range(NT):
                    dve.wait_ge(g_in[t % 2], 16 * TOPK * (t // 2 + 1))
                    for j in range(TOPK):
                        if t or j:
                            dve.wait_ge(summed, TOPK * t + j)
                        nc.vector.scalar_tensor_tensor(acc[:, t, :], gath[t % 2][:, j, :], wj[:, j, t:t + 1], acc[:, t, :], ALU.mult, ALU.add).then_inc(summed, 1)
                    dve.wait_ge(summed, TOPK * (t + 1))
                    nc.vector.bn_stats(stats[:, t, :], acc[:, t, :]).then_inc(fin_stats, 1)
                for t in range(NT):
                    dve.wait_ge(fin_stats, t + 1)
                    nc.vector.bn_aggr(mv[:, t, :], stats[:, t, :]).then_inc(fin_var, 1)
                dve.wait_ge(fin_var, NT)
                ts(veps, mv[:, :, 1], LN_EPS, None, ALU.add).then_inc(fin_r, 1)
                dve.wait_ge(fin_r, 2)
                for t in range(NT):
                    ts(acc[:, t, :], acc[:, t, :], mv[:, t, 0:1], rstd[:, t:t + 1], ALU.subtract, ALU.mult).then_inc(fin_x, 1)

            @block.sync
            def _(sp):
                for t in range(NT):
                    sp.wait_ge(fin_x, t + 1)
                    sp.dma_start(out[t * P:(t + 1) * P, :], acc[:, t, :]).then_inc(out_sem, 16)
                sp.wait_ge(out_sem, 16 * NT)


def build(nc, x_t, x_n, w_v, w_kq, w_z, prm, w_ab, rows, w_out, norm_w, consts, gate_t, w_e, xs, ys, out):
    with ExitStack() as ctx:
        cst = ctx.enter_context(nc.sbuf_tensor("cst", [P, NCONST], F32))[:]
        acc = ctx.enter_context(nc.sbuf_tensor("acc", [P, NT, HID], F32))[:]
        with nc.sbuf_tensor("zeros", [P, ZROWS * HID], F32) as zeros:
            attention(nc, cst, acc, zeros[:], x_t, x_n, w_v, w_kq, w_z, prm, w_ab, rows, w_out, norm_w, consts, xs)
        experts(nc, cst, acc, gate_t, w_e, xs, ys, out)


OUT_NAMES = ["out_0_dram"]


def kernel(**inputs):
    import numpy as np
    import concourse.bacc as bacc
    from concourse.bass_utils import run_bass_kernel_spmd as run

    a = {k[len("L0_"):]: np.asarray(v) for k, v in inputs.items()}
    x = a["attn_hidden_states"].reshape(TOK, HID)

    def by_partition(w):
        return w.reshape(KC, P, -1).transpose(1, 0, 2)

    wq, wk, wvv = np.split(a["attn_Wqkv"], [HK * P, 2 * HK * P])

    def heads(w, n):
        return w.reshape(HK, n, HID).transpose(0, 2, 1).reshape(HK, KC, P, n).transpose(0, 2, 1, 3)

    per_channel = np.concatenate([a["attn_bqkv"][:, None], a["attn_conv_b"][:, None], a["attn_conv_w"]], 1)
    cq, ck, cv = (t.reshape(HK, -1, P, NPRM) for t in np.split(per_channel, [HK * P, 2 * HK * P]))
    prm = np.concatenate([np.concatenate([cv, ck, cq], 1).transpose(0, 2, 1, 3).reshape(HK, P, 4 * NPRM),
                          a["attn_bz"].reshape(HK, REP, P).transpose(0, 2, 1)], 2)
    row = np.concatenate([a["attn_bb"], a["attn_ba"], a["attn_dt_bias"], a["attn_A_log"], a["attn_bout"]])

    r, c = np.meshgrid(np.arange(P), np.arange(P), indexing="ij")

    def joins(n, r, c):
        return (r // (2 * n) == c // (2 * n)) & (r // n % 2 == 1) & (c // n % 2 == 0)

    parts = [r == c, r <= c, r > c, r < c, r <= c, r // Q32 == c // Q32, joins(Q32, c, r)]
    parts += [joins(1 << l, r % Q32, c % Q32)[:, :Q32] for l in range(PACKED + 1)]
    parts.append((r % Q32 == c % Q32)[:, :Q32])
    parts.append(np.stack([np.arange(P), P + np.arange(P)], 1))
    masks = np.concatenate([np.asarray(m, np.float32) for m in parts], 1)
    w13 = a["ffn_w13"].reshape(NE, 2, INTER, KC, P).transpose(0, 4, 3, 1, 2).reshape(NE, P, 2 * KC * INTER)

    arrays = {
        "x_t": by_partition(x.T),
        "x_n": x.reshape(NT, P, HID).transpose(1, 0, 2),
        "w_v": heads(wvv, 2 * P),
        "w_kq": np.concatenate([heads(wk, P), heads(wq, P)], 3),
        "w_z": heads(a["attn_Wz"], 2 * P),
        "prm": prm,
        "w_ab": by_partition(np.concatenate([a["attn_Wb"], a["attn_Wa"]]).T),
        "rows": np.broadcast_to(row, (P, row.size)),
        "w_out": a["attn_Wout"].T.reshape(HV, P, HID).transpose(1, 0, 2),
        "norm_w": a["attn_norm_w"][:, None],
        "consts": masks,
        "gate_t": by_partition(a["ffn_gate_w"].T),
        "w_e": np.concatenate([w13, a["ffn_w2"].transpose(0, 2, 1)], 2),
    }
    arrays = {k: np.ascontiguousarray(v) for k, v in arrays.items()}
    nc = bacc.Bacc("TRN2", target_bir_lowering=False, num_devices=1)
    args = [nc.dram_tensor(k, v.shape, mybir.dt.from_np(v.dtype), kind="ExternalInput").ap() for k, v in arrays.items()]
    out = nc.dram_tensor("out_0_dram", (TOK, HID), F32, kind="ExternalOutput").ap()
    xs = nc.dram_tensor("pairs_in", (SLOTS, HID), F32).ap()
    ys = nc.dram_tensor("pairs_out", (SLOTS, HID), F32).ap()
    build(nc, *args, xs, ys, out)
    res = run(nc, [arrays], core_ids=[0])
    return res.results[0]["out_0_dram"].reshape(NB, SEQ, HID)
```

```python
from contextlib import ExitStack

import concourse.bass as bass
from concourse import mybir

F32 = mybir.dt.float32
I32 = mybir.dt.int32
U32 = mybir.dt.uint32
ALU = mybir.AluOpType
ACT = mybir.ActivationFunctionType

P = 128
HID = 256
KC = HID // P
NB, SEQ = 8, 256
TOK = NB * SEQ
NT = TOK // P
HK, HV = 8, 16
REP = HV // HK
PAIRS = NB // 2
ST = 2 * SEQ
TPS = ST // P
KCONV = 4
LEVELS = 6
Q32 = 32
PACKED = 4
L2_EPS = 1e-6
RMS_EPS = 1e-6
LN_EPS = 1e-5
V0, V1, K_, Q_ = range(4)
NPRM = 6
F_G, F_BETA, F_EG, F_NEG, F_DEC = range(5)
NF = 5

C_ID, C_UINC, C_LSTR, C_KKQ, C_B32, C_L32, C_LEV = 0, 128, 256, 384, 640, 768, 896
C_I32 = C_LEV + (PACKED + 1) * Q32
C_TAU = C_I32 + Q32
C_U = C_TAU + 2
NCONST = C_U + 8

NE, TOPK, INTER = 64, 8, 128
XT_TILES = (TOK * TOPK + NE * (P - 1)) // P + 1
SLOTS = XT_TILES * P
WCOL = KC * 2 * INTER + HID
U = 8
XTURNS = XT_TILES // U
HT = NT // 2
LNG = 4
assert NT % LNG == 0
UBITS = U.bit_length() - 1
assert XT_TILES % U == 0 and XT_TILES <= 2 * P and U == 1 << UBITS and UBITS * U <= 24 and NCONST == C_U + U
ZROWS = 4


class Sig:

    def __init__(self, handle, per_step, steps):
        self.handle, self.per_step, self.steps = handle, per_step, steps

    def value(self, it, i):
        turn, step = it
        return turn * (self.steps * self.per_step) + (step * self.per_step + i)


def wait(eng, sig, it, i):
    v = sig.value(it, i)
    if isinstance(v, int) and v <= 0:
        return
    eng.wait_ge(sig.handle, v)


def attention(nc, cst, acc, zeros, x_t, x_n, w_v, w_kq, w_z, prm, w_ab, rows, w_out, norm_w, consts, xs):
    with ExitStack() as ctx:
        def sb(name, *shape, dt=F32):
            return ctx.enter_context(nc.sbuf_tensor(name, [P, *shape], dt))[:]

        def bank(name):
            return ctx.enter_context(nc.psum_tensor(name, [P, 512], F32))[:]

        def sem(name):
            return ctx.enter_context(nc.semaphore(name))

        def sig(name, per_step):
            return Sig(sem(name), per_step, PAIRS)

        xT = sb("xT", KC, TOK)
        wo = sb("wo", HV, HID)
        wab = sb("wab", KC, 2 * HV)
        rowb = sb("rowb", 4 * HV + HID)
        nw = sb("nw", 1)
        ones = sb("ones", 1)
        gates = sb("gates", HK, NF * 2 * NT)
        wv = sb("wv", KC, 2 * P)
        wkq = sb("wkq", KC, 2 * P)
        wz = sb("wz", KC, 2 * P)
        pv_ = sb("pv", 2 * NPRM)
        pkq = sb("pkq", 2 * NPRM)
        pz = sb("pz", 2)
        kq = [sb(f"kq{i}", TPS, 2, P) for i in range(2)]
        vT = [sb(f"vT{i}", 2, ST) for i in range(2)]
        zT = [sb(f"zT{i}", 2, ST) for i in range(2)]
        sc = [sb(f"sc{i}", NF, 2 * TPS) for i in range(2)]
        b2 = [sb(f"b2{i}", 2 * TPS) for i in range(2)]
        epsq = [sb(f"epsq{i}", TPS) for i in range(2)]
        irt = [sb(f"irt{i}", TPS) for i in range(2)]
        PT = [sb(f"PT{i}", 2, 4, P) for i in range(2)]
        raw = [sb(f"raw{i}", 2, KCONV - 1 + SEQ) for i in range(2)]
        yc = [sb(f"yc{i}", 2, SEQ) for i in range(2)]
        th = [sb(f"th{i}", ST) for i in range(2)]
        zr = [sb(f"zr{i}", ST) for i in range(2)]
        zth = [sb(f"zth{i}", ST) for i in range(2)]
        ksq = sb("ksq", TPS, 2, P)
        kss_k = sb("kss_k", TPS)
        kss_h = sb("kss_h", TPS)
        rcp = sb("rcp", TPS)
        ms = sb("ms", 2 * 4)
        msb = sb("msb", 2 * 4)
        rO = sb("rO", 2 * 4)
        expo = sb("expo", 2, 8)
        gm = sb("gm", 2, 4, P)
        E = sb("E", 2, 4, P)
        kkqm = sb("kkqm", 2, 2, 2, P)
        LT = sb("LT", 2, 4, P)
        LTD = sb("LTD", 2, 4, P)
        LT4 = sb("LT4", 2, 4, P)
        Xp = sb("Xp", 2, 4, Q32)
        XTp = sb("XTp", 2, 4, Q32)
        XT = sb("XT", 2, 4, P)
        T1p = sb("T1p", 2, 4, Q32)
        T1F = sb("T1F", 2, 4, P)
        X64 = sb("X64", 2, 4, 64)
        T15 = sb("T15", 2, 4, 64)
        XTF = sb("XTF", 2, 4, P)
        vn = sb("vn", 2, 4, P)
        kn = sb("kn", 2, P)
        dl = sb("dl", 2, 4, P)
        dec = sb("dec", 2, 2, P)
        ssb = sb("ssb", 2, 2 * P)
        w1 = sb("w1", 2, 2, P)
        qse = sb("qse", 2, 2, P)
        osb = sb("osb", 2, 4, P)
        osc = sb("osc", 2, 4, P)
        gT = sb("gT", 2, 4, P)

        SB = [bank(f"solve{g}") for g in range(2)]
        PB = [bank(f"proj{i}") for i in range(2)]
        A = [bank(f"tailA{g}") for g in range(2)]
        B = [bank(f"tailB{g}") for g in range(2)]

        in_const, in_x0, in_x, in_acc, in_misc, in_wo = (sem(n) for n in ("in_const", "in_x0", "in_x", "in_acc", "in_misc", "in_wo"))
        in_wv, in_wkq, in_wz = sem("in_wv"), sem("in_wkq"), sem("in_wz")
        wo_scaled, acc_biased = sem("wo_scaled"), sem("acc_biased")
        set_pool, set_dve, set_act, set_pe = sem("set_pool"), sem("set_dve"), sem("set_act"), sem("set_pe")
        kkq, diff = sig("kkq", 2), sig("diff", 2)
        t1, xu = sig("t1", 2 * LEVELS), sig("xu", 2 * LEVELS)
        d0, s0, ksqs, d1, o_, ot, wo_ = (sig(n, 2) for n in ("d0", "s0", "ksqs", "d1", "o", "ot", "wo_d"))
        proj, zproj, kss = sig("proj", 4), sig("zproj", 2), sig("kss", 1)
        vt, knt = sig("vt", 2), sig("knt", 2)
        exp_, dl0, ssev, rawd, tap3, tanh = sig("exp", 2), sig("dl0", 2), sig("ssev", 2), sig("raw_d", 4), sig("tap3", 4), sig("tanh", 4)
        zraw, ztanh, qsed, dl1 = sig("zraw", 2), sig("ztanh", 2), sig("qse_d", 2), sig("dl1", 2)
        xeA, ltdA, t1a, xtc, x64a = sig("xeA", PACKED + 1), sig("ltdA", 1), sig("t1a", 4), sig("xtc", 2), sig("x64a", 2)
        sqd, vnd, knd, ksqd = sig("sqd", 2), sig("vnd", 2), sig("knd", 2), sig("ksqd", 1)
        kkqd, kssd, rcpd, b2d, decd, ltd, xp0 = sig("kkqd", 2), sig("kssd", 1), sig("rcpd", 1), sig("b2d", 1), sig("decd", 2), sig("ltd", 2), sig("xp0", 4)
        xd, xtpd, t1d, offd, xtfd = sig("xd", 2 * PACKED + 2), sig("xtpd", 2 * PACKED + 2), sig("t1d", 2 * PACKED), sig("offd", 4), sig("xtfd", 2)
        taps, silu, zsilu = sig("taps", 12), sig("silu", 4), sig("zsilu", 2)
        w1d, osbd, msd, oscd, gtd, accd, scd = sig("w1d", 2), sig("osbd", 2), sig("msd", 1), sig("oscd", 2), sig("gtd", 2), sig("accd", 2), sig("scd", 1)
        irtd, ptd, rOd, gmd = sig("irtd", 1), sig("ptd", 2), sig("rOd", 1), sig("gmd", 2)
        ltdP, lt4d, xeP = sig("ltdP", 1), sig("lt4d", 2), sig("xeP", PACKED + 1)
        zeroed = sem("zeroed")
        of_set_up = [t.rearrange("p g a t -> p (g a t)")[:, n * NT * HV:(n + 1) * NT * HV].rearrange("p (t h) -> p t h", h=HV)
                     for t, n in ((osb, 0), (osb, 1), (osb, 2), (osb, 3), (gT, 0), (gT, 1))]
        ga, gb, gab, ge, gl, gg = of_set_up
        rowa = sb("rowa", HV)
        eal = sb("eal", HV)

        ident = cst[:, C_ID:C_ID + P]
        uinc = cst[:, C_UINC:C_UINC + P]
        lstr = cst[:, C_LSTR:C_LSTR + P]

        def rep4(c):
            return cst[:, c:c + P].unsqueeze(1).to_broadcast([P, 4, P])

        def rep_packed(c):
            return cst[:, c:c + Q32].unsqueeze(1).to_broadcast([P, 4, Q32])

        def quad(t, g, b, n=1, cols=None):
            t = t[b * Q32:(b + n) * Q32, g]
            return t if cols is None else t[:, :, cols * Q32:(cols + n) * Q32]

        def packed_psum(g, i, b=0, n=4):
            return SB[g][b * Q32:(b + n) * Q32, i * P:(i + 1) * P].rearrange("p (a t) -> p a t", a=4)

        def prm_of(c):
            t = (pv_ if c in (V0, V1) else pkq)[:, (c % 2) * NPRM:(c % 2 + 1) * NPRM]
            return t

        def col(t, i):
            return t[:, i:i + 1]

        def dst_of(c, p):
            if c in (V0, V1):
                return vT[p][:, c, :].rearrange("p (n t) -> p n t", t=P)
            return kq[p][:, :, c - K_, :]

        def g_col(p, f, g, v, c):
            i = (2 * g + c) * 2 + v
            return sc[p][:, f, i:i + 1]

        def b2_col(p, g, v, c):
            i = (2 * g + c) * 2 + v
            return b2[p][:, i:i + 1]

        block = ctx.enter_context(nc.Block())
        LAST = (HK - 1, PAIRS - 1)

        def run_steps(eng, step):
            for pair in range(PAIRS):
                step((0, pair), first=pair == 0, last=False)
            with eng.Fori(1, HK - 1) as hk:
                for pair in range(PAIRS):
                    step((hk, pair), first=False, last=False)
            for pair in range(PAIRS):
                step((HK - 1, pair), first=False, last=pair == PAIRS - 1)

        @block.sync
        def _(sp):
            def load_head(hk, part):
                if part == 0:
                    sp.dma_start(wv, w_v[bass.ds(hk, 1)].rearrange("a p k n -> p (a k) n")).then_inc(in_wv, 16)
                    sp.dma_start(pv_, prm[bass.ds(hk, 1), :, 0:12].rearrange("a p n -> p (a n)")).then_inc(in_wv, 16)
                elif part == 1:
                    sp.dma_start(wkq, w_kq[bass.ds(hk, 1)].rearrange("a p k n -> p (a k) n")).then_inc(in_wkq, 16)
                    sp.dma_start(pkq, prm[bass.ds(hk, 1), :, 12:24].rearrange("a p n -> p (a n)")).then_inc(in_wkq, 16)
                else:
                    sp.dma_start(wz, w_z[bass.ds(hk, 1)].rearrange("a p k n -> p (a k) n")).then_inc(in_wz, 16)
                    sp.dma_start(pz, prm[bass.ds(hk, 1), :, 24:26].rearrange("a p n -> p (a n)")).then_inc(in_wz, 16)

            load_head(0, 0)
            sp.dma_start(xT[:, :, 0:ST], x_t[:, :, 0:ST]).then_inc(in_x0, 16)
            for s, t in ((w_ab, wab), (rows, rowb), (norm_w, nw)):
                sp.dma_start(t, s).then_inc(in_misc, 16)
            sp.dma_start(xT[:, :, ST:], x_t[:, :, ST:]).then_inc(in_x, 16)
            load_head(0, 1)
            sp.dma_start(cst, consts).then_inc(in_const, 16)
            sp.dma_start(wo, w_out).then_inc(in_wo, 16)
            load_head(0, 2)
            sp.dma_start(acc, x_n).then_inc(in_acc, 16)
            sp.wait_ge(set_pool, 1)
            for n in range(SLOTS // (P * ZROWS)):
                sp.dma_start(xs[n * P * ZROWS:(n + 1) * P * ZROWS, :].rearrange("(p a) n -> p (a n)", p=P), zeros).then_inc(zeroed, 16)
            with sp.Fori(0, HK - 1) as hk:
                wait(sp, silu, (hk, PAIRS - 1), 2)
                load_head(hk + 1, 0)
                wait(sp, silu, (hk, PAIRS - 1), 4)
                load_head(hk + 1, 1)
                wait(sp, zraw, (hk, PAIRS - 1), 2)
                load_head(hk + 1, 2)
            sp.wait_ge(zeroed, 16 * (SLOTS // (P * ZROWS)))

        @block.tensor
        def _(pe):
            mm = nc.tensor.matmul

            def project(nx, c, parts=range(KC)):
                w_ = wv if c in (V0, V1) else wkq
                for k in parts:
                    last = mm(PB[c % 2], w_[:, k, (c % 2) * P:(c % 2 + 1) * P],
                              xT[:, k, (nx[1] % PAIRS) * ST:(nx[1] % PAIRS + 1) * ST], start=k == 0, stop=k == KC - 1)
                if KC - 1 in parts:
                    last.then_inc(proj.handle, 1)

            def products(nx, p):
                for g in range(2):
                    wait(pe, silu, nx, 4)
                    wait(pe, zraw, (nx[0], nx[1] - 1), g + 1)
                    for c in range(2):
                        tile = kq[p][:, 2 * g + c, :, :]
                        m = mm(PB[g][:, c * 256:(c + 1) * 256], tile[:, 0, :], tile.rearrange("p a t -> p (a t)"), start=True, stop=True)
                    m.then_inc(kkq.handle, 1)

            def head_of(nx):
                return nx[0] + nx[1] // PAIRS

            def weights_in(s, hk):
                pe.wait_ge(s, hk * 32 + 32)

            def tail_d0(pv):
                for g in range(2):
                    wait(pe, vnd, pv, g + 1)
                    wait(pe, xtfd, pv, g + 1)
                    for v in range(2):
                        m = mm(A[g][:, v * P:(v + 1) * P], XTF[:, g, 2 * v, :], vn[:, g, 2 * v, :], start=True, stop=True)
                    m.then_inc(d0.handle, 1)

            def tail_s0(pv):
                for g in range(2):
                    wait(pe, decd, pv, g + 1)
                    wait(pe, knd, pv, g + 1)
                    mm(B[g][:, 0:256], kn[:, g, :], dec[:, g].rearrange("p a t -> p (a t)"), start=True, stop=True).then_inc(s0.handle, 1)

            def tail_ksqs(pv, q):
                for g in range(2):
                    wait(pe, ssev, pv, g + 1)
                    rhs = ssb[:, g, :]
                    mm(A[g][:, 256:512], kq[q][:, 2 * g + 1, 0, :], rhs, start=True, stop=True)
                    mm(B[g][:, 256:512], kq[q][:, 2 * g + 1, 1, :], rhs, start=True, stop=True).then_inc(ksqs.handle, 1)

            def tail_d1(pv):
                for g in range(2):
                    wait(pe, w1d, pv, g + 1)
                    for v in range(2):
                        m = mm(A[g][:, v * P:(v + 1) * P], XTF[:, g, 2 * v + 1, :], w1[:, g, v, :], start=True, stop=True)
                    m.then_inc(d1.handle, 1)

            def tail_o(pv, q):
                for g in range(2):
                    wait(pe, dl1, pv, g + 1)
                    wait(pe, qsed, pv, g + 1)
                    for i in range(4):
                        m = mm(B[g][:, i * P:(i + 1) * P], PT[q][:, g, i, :], dl[:, g, i, :], start=True, stop=True)
                    m.then_inc(o_.handle, 1)

            def tail_ot(pv):
                for g in range(2):
                    wait(pe, oscd, pv, g + 1)
                    for i in range(4):
                        m = nc.tensor.transpose(A[g][:, i * P:(i + 1) * P], osc[:, g, i, :], ident)
                    m.then_inc(ot.handle, 1)

            def tail_wo(pv):
                hk = pv[0] + pv[1] // PAIRS
                if isinstance(pv[0], int) and pv == (0, 0):
                    pe.wait_ge(wo_scaled, 1)
                for g in range(2):
                    wait(pe, gtd, pv, g + 1)
                    for c in range(2):
                        for v in range(2):
                            m = mm(B[g][:, c * 256:(c + 1) * 256], gT[:, g, 2 * v + c, :],
                                   wo.rearrange("p h n -> p (h n)")[:, bass.ds((hk * REP + v) * HID, HID)], start=v == 0, stop=v == 1)
                    m.then_inc(wo_.handle, 1)

            def step(it, first, last):
                hk, pair = it
                p, q = pair % 2, 1 - pair % 2
                nx, pv = (hk, pair + 1), (hk, pair - 1)
                xs = slice(pair * ST, (pair + 1) * ST)
                tail = not first

                wait(pe, ksqd, it, 1)
                wait(pe, kkqd, it, 2)
                for i in range(2 * TPS):
                    mmi = mm(PB[0][:, i:i + 1], ksq[:, i // 2, i % 2, :], ones, start=True, stop=True)
                mmi.then_inc(kss.handle, 1)
                for g in range(2):
                    wait(pe, gmd, it, g + 1)
                    wait(pe, xtfd, pv, g + 1)
                    mm(SB[g], lstr, gm[:, g].rearrange("p a t -> p (a t)"), start=True, stop=True).then_inc(diff.handle, 1)
                if tail:
                    tail_d0(pv)

                def level_t1(l):
                    for g in range(2):
                        if l == 0:
                            wait(pe, (ltdP, ltdA)[g], it, 1)
                        if l < PACKED:
                            wait(pe, xd, it, 2 * l + g + 1)
                        elif l == PACKED:
                            wait(pe, xd, it, 2 * l + g + 1)
                            wait(pe, lt4d, it, g + 1)
                        else:
                            wait(pe, offd, it, 2 + g + 1)
                            wait(pe, x64a, it, g + 1)
                        for i in range(4):
                            if l <= PACKED:
                                m = mm(SB[g][:, i * Q32:(i + 1) * Q32], (LTD if l < PACKED else LT4)[:, g, i, :], Xp[:, g, i, :], start=True, stop=True)
                            else:
                                m = mm(SB[g][:, i * 64:(i + 1) * 64], LT[0:64, g, i, :], X64[0:64, g, i, :], start=True, stop=True)
                        m.then_inc(t1.handle, 1)

                def level_xu(l):
                    for g in range(2):
                        if l < PACKED:
                            wait(pe, t1d, it, 2 * l + g + 1)
                            wait(pe, (xeP, xeA)[g], it, l + 1)
                            for i in range(4):
                                m = mm(SB[g][:, P + i * Q32:P + (i + 1) * Q32], XT[:, g, i, :], T1p[:, g, i, :], start=True, stop=True)
                        elif l == PACKED:
                            wait(pe, t1a, it, g + 1)
                            wait(pe, xtpd, it, 2 * PACKED + g + 1)
                            for i in range(4):
                                m = mm(SB[g][:, P + i * Q32:P + (i + 1) * Q32], T1F[:, g, i, :], XTp[:, g, i, :], start=True, stop=True)
                        else:
                            wait(pe, t1a, it, 2 + g + 1)
                            for i in range(4):
                                m = mm(SB[g][0:64, 256 + i * 64:256 + (i + 1) * 64], T15[:, g, i, :], XTF[:, g, i, 64:128], start=True, stop=True)
                        m.then_inc(xu.handle, 1)

                def project_z(v, parts):
                    for k in parts:
                        m = mm(PB[v], wz[:, k, v * P:(v + 1) * P], xT[:, k, xs], start=k == 0, stop=k == KC - 1)
                    if KC - 1 in parts:
                        m.then_inc(zproj.handle, 1)

                if not last:
                    weights_in(in_wv, head_of(nx))
                    wait(pe, kssd, it, 1)
                    project(nx, V0)
                if tail:
                    tail_s0(pv)
                if not last:
                    project(nx, V1)
                if tail:
                    tail_ksqs(pv, q)
                level_t1(0)
                if tail:
                    tail_d1(pv)
                level_xu(0)
                if not last:
                    weights_in(in_wkq, head_of(nx))
                    wait(pe, rawd, nx, V0 + 1)
                    project(nx, K_)
                level_t1(1)
                if tail:
                    tail_o(pv, q)
                level_xu(1)
                if not last:
                    wait(pe, rawd, nx, V1 + 1)
                    project(nx, Q_)
                level_t1(2)
                weights_in(in_wz, hk)
                if not last:
                    wait(pe, rawd, nx, K_ + 1)
                else:
                    wait(pe, kssd, it, 1)
                project_z(0, [0])
                level_xu(2)
                project_z(0, [1])
                level_t1(3)
                if not last:
                    wait(pe, rawd, nx, Q_ + 1)
                project_z(1, [0])
                level_xu(3)
                project_z(1, [1])
                if tail:
                    tail_ot(pv)
                level_t1(4)
                level_xu(4)
                if tail:
                    tail_wo(pv)
                level_t1(5)
                for g in range(2):
                    for v in range(2):
                        for c in range(2):
                            t = 2 * g + c
                            m = nc.tensor.transpose(A[g][:, (2 * v + c) * P:(2 * v + c + 1) * P], vT[p][:, v, t * P:(t + 1) * P], ident)
                    m.then_inc(vt.handle, 1)
                if not last:
                    products(nx, q)
                for g in range(2):
                    if tail:
                        wait(pe, accd, pv, g + 1)
                    nc.tensor.transpose(B[g][:, 0:P], kq[p][:, 2 * g, 0, :], ident).then_inc(knt.handle, 1)
                level_xu(5)

            def final_tail():
                q = LAST[1] % 2
                tail_d0(LAST)
                tail_s0(LAST)
                tail_ksqs(LAST, q)
                tail_d1(LAST)
                tail_o(LAST, q)
                tail_ot(LAST)
                tail_wo(LAST)

            pe.wait_ge(in_x0, 16)
            weights_in(in_wv, 0)
            project((0, 0), V0)
            project((0, 0), V1)
            pe.wait_ge(in_x, 16)
            pe.wait_ge(in_misc, 48)
            for t in range(NT):
                for k in range(KC):
                    m = mm(SB[0][:, t * 32:(t + 1) * 32], xT[:, k, t * P:(t + 1) * P], wab[:, k, :], start=k == 0, stop=k == KC - 1)
            m.then_inc(set_pe, 1)
            weights_in(in_wkq, 0)
            for c in (K_, Q_):
                wait(pe, rawd, (0, 0), c - 1)
                project((0, 0), c)
            pe.wait_ge(in_const, 16)
            pe.wait_ge(set_dve, 5)
            mm(A[0][:, 0:256], uinc, gg.rearrange("p t h -> p (t h)"), start=True, stop=True)
            mm(A[1][:, 0:256], lstr, gg.rearrange("p t h -> p (t h)"), start=True, stop=True).then_inc(set_pe, 1)
            pe.wait_ge(set_act, 5)
            products((0, 0), 0)
            run_steps(pe, step)
            final_tail()

        @block.scalar
        def _(act):
            av = nc.scalar.activation

            def conv_in(nx, c):
                pr = prm_of(c)
                wait(act, proj, nx, c + 1)
                wait(act, taps, nx, 3 * (c - 1))
                av(raw[c % 2][:, :, KCONV - 1:], PB[c % 2].rearrange("p (b t) -> p b t", b=2), ACT.Identity, bias=col(pr, 0)).then_inc(rawd.handle, 1)
                wait(act, silu, nx, c - 1)
                wait(act, rawd, nx, c + 1)
                av(yc[c % 2], raw[c % 2][:, :, KCONV - 1:], ACT.Identity, bias=col(pr, 1), scale=col(pr, 5)).then_inc(tap3.handle, 1)

            def conv_tanh(nx, c):
                wait(act, taps, nx, 3 * (c + 1))
                av(th[c % 2], yc[c % 2].rearrange("p b t -> p (b t)"), ACT.Tanh, scale=0.5).then_inc(tanh.handle, 1)

            def z_in(it, v):
                wait(act, zproj, it, v + 1)
                wait(act, zsilu, it, v - 1)
                av(zr[v], PB[v], ACT.Identity, bias=col(pz, v)).then_inc(zraw.handle, 1)
                wait(act, zraw, it, v + 1)
                av(zth[v], zr[v], ACT.Tanh, scale=0.5).then_inc(ztanh.handle, 1)

            def ltd_out(it):
                wait(act, ltd, it, 2)
                for b in range(4):
                    a = av(quad(LTD, 1, b, cols=b), quad(LT, 1, b, cols=b), ACT.Copy)
                a.then_inc(ltdA.handle, 1)

            def xt_expand(it, l):
                wait(act, xtpd, it, 2 * l + 2)
                for b in range(4):
                    a = av(quad(XT, 1, b, cols=b), quad(XTp, 1, b), ACT.Copy)
                a.then_inc(xeA.handle, 1)

            def t1_out4(it):
                for g in range(2):
                    wait(act, t1, it, 2 * PACKED + g + 1)
                    for b in (1, 3):
                        a = av(quad(T1F, g, b, cols=b - 1), packed_psum(g, 0, b, 1), ACT.Copy)
                    a.then_inc(t1a.handle, 1)

            def x64_out(it):
                for g in range(2):
                    wait(act, (xeP, xeA)[g], it, PACKED + 1)
                    av(XTF[:, g], XT[:, g], ACT.Copy).then_inc(xtc.handle, 1)
                    for b in (0, 1):
                        a = av(quad(X64, g, b, cols=b), quad(Xp, g, b), ACT.Copy)
                    a.then_inc(x64a.handle, 1)

            def t1_out5(it):
                for g in range(2):
                    wait(act, t1, it, 2 * LEVELS - 2 + g + 1)
                    av(T15[64:128, g], SB[g][64:128, 0:256].rearrange("p (a t) -> p a t", a=4), ACT.Copy).then_inc(t1a.handle, 1)

            def square(nx, p):
                wait(act, silu, nx, 4)
                av(ksq, kq[p], ACT.Square).then_inc(ksqd.handle, 1)

            def t_dl0(pv, q):
                for g in range(2):
                    wait(act, d0, pv, g + 1)
                    for v in range(2):
                        a = av(dl[:, g, 2 * v, :], A[g][:, v * P:(v + 1) * P], ACT.Copy, scale=b2_col(q, g, v, 0))
                    a.then_inc(dl0.handle, 1)

            def t_dec(pv, q):
                for g in range(2):
                    wait(act, dl0, pv, g + 1)
                    for v in range(2):
                        a = av(dec[:, g, v, :], dl[:, g, 2 * v, :], ACT.Copy, scale=g_col(q, F_DEC, g, v, 0))
                    a.then_inc(decd.handle, 1)

            def t_state(pv):
                for g in range(2):
                    wait(act, s0, pv, g + 1)
                    av(ssb[:, g, :], B[g][:, 0:256], ACT.Copy).then_inc(ssev.handle, 1)

            def t_qse(pv, q):
                for g in range(2):
                    wait(act, ksqs, pv, g + 1)
                    for v in range(2):
                        a = av(qse[:, g, v, :], B[g][:, 256 + v * P:256 + (v + 1) * P], ACT.Copy, scale=g_col(q, F_EG, g, v, 1))
                    a.then_inc(qsed.handle, 1)

            def t_dl1(pv, q):
                for g in range(2):
                    wait(act, d1, pv, g + 1)
                    for v in range(2):
                        a = av(dl[:, g, 2 * v + 1, :], A[g][:, v * P:(v + 1) * P], ACT.Copy, scale=b2_col(q, g, v, 1))
                    a.then_inc(dl1.handle, 1)

            def t_square(pv):
                for g in range(2):
                    wait(act, osbd, pv, g + 1)
                    for i in range(4):
                        a = av(osc[:, g, i, :], osb[:, g, i, :], ACT.Square, accum_out=ms[:, 4 * g + i:4 * g + i + 1])
                    a.then_inc(sqd.handle, 1)

            def step(it, first, last):
                hk, pair = it
                p, q = pair % 2, 1 - pair % 2
                nx, pv = (hk, pair + 1), (hk, pair - 1)
                tail = not first
                for g in range(2):
                    wait(act, diff, it, g + 1)
                    wait(act, ptd, pv, g + 1)
                    av(E[:, g].rearrange("p a t -> p (a t)"), SB[g], ACT.Exp).then_inc(exp_.handle, 1)
                if tail:
                    t_dl0(pv, q)
                    t_dec(pv, q)
                if not last:
                    if pair == PAIRS - 1:
                        act.wait_ge(in_wv, (hk + 1) * 32 + 32)
                    conv_in(nx, V0)
                if tail:
                    t_state(pv)
                ltd_out(it)
                if tail:
                    t_qse(pv, q)
                xt_expand(it, 0)
                if not last:
                    conv_tanh(nx, V0)
                    conv_in(nx, V1)
                if tail:
                    t_dl1(pv, q)
                xt_expand(it, 1)
                if not last:
                    if pair == PAIRS - 1:
                        act.wait_ge(in_wkq, (hk + 1) * 32 + 32)
                    conv_in(nx, K_)
                    conv_tanh(nx, V1)
                xt_expand(it, 2)
                if tail:
                    t_square(pv)
                if not last:
                    conv_tanh(nx, K_)
                    conv_in(nx, Q_)
                xt_expand(it, 3)
                if pair == 0:
                    act.wait_ge(in_wz, hk * 32 + 32)
                z_in(it, 0)
                if not last:
                    conv_tanh(nx, Q_)
                z_in(it, 1)
                t1_out4(it)
                xt_expand(it, 4)
                x64_out(it)
                t1_out5(it)
                if not last:
                    square(nx, q)
                for g in range(2):
                    wait(act, vt, it, g + 1)
                    wait(act, irtd, it, 1)
                    for v in range(2):
                        for c in range(2):
                            t = 2 * g + c
                            a = av(vn[:, g, 2 * v + c, :], A[g][:, (2 * v + c) * P:(2 * v + c + 1) * P], ACT.Copy, scale=irt[p][:, t:t + 1])
                    a.then_inc(vnd.handle, 1)
                for g in range(2):
                    wait(act, knt, it, g + 1)
                    av(kn[:, g, :], B[g][:, 0:P], ACT.Copy).then_inc(knd.handle, 1)

            act.wait_ge(in_wv, 32)
            for c in (V0, V1):
                conv_in((0, 0), c)
            for c in (V0, V1):
                conv_tanh((0, 0), c)
            act.wait_ge(in_wkq, 32)
            for c in (K_, Q_):
                conv_in((0, 0), c)
            act.wait_ge(set_dve, 2)
            act.wait_ge(in_misc, 48)
            av(ge, gab, ACT.Exp, scale=-1.0)
            av(eal, rowb[:, 3 * HV:4 * HV], ACT.Exp).then_inc(set_act, 1)
            act.wait_ge(set_act, 1)
            av(gl, ge, ACT.Ln, bias=1.0).then_inc(set_act, 1)
            act.wait_ge(set_dve, 3)
            av(gb, gb, ACT.Tanh, scale=0.5).then_inc(set_act, 1)
            for c in (K_, Q_):
                conv_tanh((0, 0), c)
            square((0, 0), 0)

            def field(f):
                return gates.rearrange("p h (f t v) -> p h f t v", f=NF, v=2)[:, :, f]

            act.wait_ge(set_pe, 2)
            for h in range(HK):
                av(field(F_EG)[:, h], A[0][:, 0:256].rearrange("p (t h v) -> p h t v", h=HK, v=2)[:, h], ACT.Exp)
                a = av(field(F_DEC)[:, h], A[1][:, 0:256].rearrange("p (t h v) -> p h t v", h=HK, v=2)[:, h], ACT.Exp)
            a.then_inc(set_act, 2)
            run_steps(act, step)
            t_dl0(LAST, 1)
            t_dec(LAST, 1)
            t_state(LAST)
            t_qse(LAST, 1)
            t_dl1(LAST, 1)
            t_square(LAST)

        @block.vector
        def _(dve):
            tt, stt, ts = nc.vector.tensor_tensor, nc.vector.scalar_tensor_tensor, nc.vector.tensor_scalar

            def conv_taps(nx, c):
                pr = prm_of(c)
                y = yc[c % 2]
                wait(dve, rawd, nx, c + 1)
                wait(dve, tap3, nx, c + 1)
                for j in range(KCONV - 1):
                    if j:
                        wait(dve, taps, nx, 3 * c + j)
                    stt(y, raw[c % 2][:, :, j:j + SEQ], col(pr, 2 + j), y, ALU.mult, ALU.add).then_inc(taps.handle, 1)

            def conv_silu(nx, c, p):
                wait(dve, tanh, nx, c + 1)
                stt(dst_of(c, p), th[c % 2].rearrange("p (n t) -> p n t", t=P), 1.0,
                    yc[c % 2].rearrange("p b (n t) -> p (b n) t", t=P), ALU.add, ALU.mult).then_inc(silu.handle, 1)

            def z_silu(it, v, p):
                wait(dve, ztanh, it, v + 1)
                stt(zT[p][:, v, :], zth[v], 1.0, zr[v], ALU.add, ALU.mult).then_inc(zsilu.handle, 1)

            def gates_of(nx, p):
                hk, pair = nx[0] + nx[1] // PAIRS, nx[1] % PAIRS
                src = gates.rearrange("p h (f t) -> p h f t", f=NF)[:, bass.ds(hk, 1), :, pair * 2 * TPS:(pair + 1) * 2 * TPS]
                tt(sc[p], src.rearrange("p h f t -> p (h f) t"), src.rearrange("p h f t -> p (h f) t"), ALU.max).then_inc(scd.handle, 1)

            def t1_out(it, l):
                for g in range(2):
                    wait(dve, t1, it, 2 * l + g + 1)
                    tt(T1p[:, g], packed_psum(g, 0), rep_packed(C_LEV + (l + 1) * Q32), ALU.mult).then_inc(t1d.handle, 1)

            def x_start(it):
                for g in range(2):
                    wait(dve, ltd, it, g + 1)
                    for b in range(4):
                        a = nc.vector.transpose(quad(Xp, g, b), quad(LT, g, b, cols=b))
                    a.then_inc(xp0.handle, 1)
                for g in range(2):
                    wait(dve, xp0, it, g + 1)
                    tt(Xp[:, g], Xp[:, g], rep_packed(C_LEV), ALU.mult).then_inc(xp0.handle, 1)
                for g in range(2):
                    wait(dve, xp0, it, 2 + g + 1)
                    tt(Xp[:, g], rep_packed(C_I32), Xp[:, g], ALU.subtract).then_inc(xd.handle, 1)

            def xtp_out(it, l):
                for g in range(2):
                    wait(dve, xd, it, 2 * l + g + 1)
                    nc.vector.transpose(XTp[:, g], Xp[:, g]).then_inc(xtpd.handle, 1)

            def x_out(it, l):
                for g in range(2):
                    wait(dve, xu, it, 2 * l + g + 1)
                    tt(Xp[:, g], Xp[:, g], packed_psum(g, 1), ALU.subtract).then_inc(xd.handle, 1)
                xtp_out(it, l + 1)

            def x_out4(it):
                for g in range(2):
                    wait(dve, xu, it, 2 * PACKED + g + 1)
                    wait(dve, xtc, it, g + 1)
                    for b in (0, 2):
                        a = ts(quad(XTF, g, b)[:, :, (b + 1) * Q32:(b + 2) * Q32], packed_psum(g, 1, b, 1), -1.0, None, ALU.mult)
                    a.then_inc(offd.handle, 1)
                for g in range(2):
                    wait(dve, offd, it, g + 1)
                    nc.vector.transpose(quad(X64, g, 1, cols=0), quad(XTF, g, 0, cols=1)).then_inc(offd.handle, 1)

            def x_out5(it):
                for g in range(2):
                    wait(dve, xu, it, 2 * LEVELS - 2 + g + 1)
                    ts(XTF[0:64, g, :, 64:128], SB[g][0:64, 256:512].rearrange("p (a t) -> p a t", a=4), -1.0, None, ALU.mult).then_inc(xtfd.handle, 1)

            def products_out(nx):
                for g in range(2):
                    wait(dve, kkq, nx, g + 1)
                    wait(dve, ptd, (nx[0], nx[1] - 1), g + 1)
                    tt(kkqm[:, g].rearrange("p c a t -> p c (a t)"), PB[g].rearrange("p (c n) -> p c n", c=2),
                       cst[:, C_KKQ:C_KKQ + 256].unsqueeze(1).to_broadcast([P, 2, 256]), ALU.mult).then_inc(kkqd.handle, 1)

            def t_w1(pv, q):
                for g in range(2):
                    wait(dve, ksqs, pv, g + 1)
                    for v in range(2):
                        a = stt(w1[:, g, v, :], A[g][:, 256 + v * P:256 + (v + 1) * P], g_col(q, F_NEG, g, v, 1), vn[:, g, 2 * v + 1, :], ALU.mult, ALU.add)
                    a.then_inc(w1d.handle, 1)

            def t_osb(pv):
                for g in range(2):
                    wait(dve, o_, pv, g + 1)
                    wait(dve, qsed, pv, g + 1)
                    ov = osb[:, g].rearrange("p (v c) t -> p v c t", v=2)
                    bv = B[g].rearrange("p (v c t) -> p v c t", v=2, c=2)
                    nc.vector.tensor_copy(ov[:, :, 0], bv[:, :, 0])
                    tt(ov[:, :, 1], bv[:, :, 1], qse[:, g], ALU.add).then_inc(osbd.handle, 1)

            def t_ms(pv, q):
                wait(dve, sqd, pv, 2)
                ep = epsq[q].rearrange("p (g c) -> p g c", g=2)
                for g in range(2):
                    a = stt(msb[:, 4 * g:4 * g + 4].rearrange("p (v c) -> p v c", v=2), ms[:, 4 * g:4 * g + 4].rearrange("p (v c) -> p v c", v=2),
                            4.0 / P, ep[:, g].unsqueeze(1).to_broadcast([P, 2, 2]), ALU.mult, ALU.add)
                a.then_inc(msd.handle, 1)

            def t_gate(pv, q):
                for g in range(2):
                    wait(dve, ot, pv, g + 1)
                    tt(gT[:, g].rearrange("p (v c) t -> p v (c t)", v=2), A[g].rearrange("p (v n) -> p v n", v=2),
                       zT[q][:, :, g * SEQ:(g + 1) * SEQ], ALU.mult).then_inc(gtd.handle, 1)

            def t_acc(pv):
                pr = pv[1] % PAIRS
                if isinstance(pv[0], int) and pv == (0, 0):
                    dve.wait_ge(acc_biased, 1)
                for g in range(2):
                    wait(dve, wo_, pv, g + 1)
                    a_ = acc[:, pr * TPS + 2 * g:pr * TPS + 2 * g + 2, :]
                    tt(a_, a_, B[g].rearrange("p (c n) -> p c n", c=2), ALU.add).then_inc(accd.handle, 1)

            def step(it, first, last):
                hk, pair = it
                p, q = pair % 2, 1 - pair % 2
                nx, pv = (hk, pair + 1), (hk, pair - 1)
                tail = not first
                wait(dve, kss, it, 1)
                ksv = PB[0][:, 0:2 * TPS].rearrange("p (t a) -> p a t", a=2)
                ts(kss_k, ksv[:, 0], 4 * L2_EPS, None, ALU.add)
                ts(kss_h, ksv[:, 0], 4 * L2_EPS, 0.25, ALU.add, ALU.mult)
                ts(epsq[p], ksv[:, 1], 4 * L2_EPS, 4 * RMS_EPS * P, ALU.add, ALU.mult).then_inc(kssd.handle, 1)
                wait(dve, kssd, it, 1)
                nc.vector.reciprocal(rcp, kss_k).then_inc(rcpd.handle, 1)
                wait(dve, rcpd, it, 1)
                tt(b2[p].rearrange("p (t v) -> p t v", v=2), sc[p][:, F_BETA].rearrange("p (t v) -> p t v", v=2),
                   rcp.unsqueeze(2).to_broadcast([P, TPS, 2]), ALU.mult).then_inc(b2d.handle, 1)
                wait(dve, b2d, it, 1)
                for g in range(2):
                    wait(dve, exp_, it, g + 1)
                    for v in range(2):
                        for c in range(2):
                            a = stt(LT[:, g, 2 * v + c, :], kkqm[:, g, c, 0, :], b2_col(p, g, v, c), E[:, g, 2 * v + c, :], ALU.mult, ALU.mult)
                    a.then_inc(ltd.handle, 1)
                x_start(it)
                xtp_out(it, 0)
                if tail:
                    t_w1(pv, q)
                t1_out(it, 0)
                if not last:
                    conv_taps(nx, V0)
                x_out(it, 0)
                t1_out(it, 1)
                if not last:
                    conv_silu(nx, V0, q)
                    conv_taps(nx, V1)
                x_out(it, 1)
                if tail:
                    t_osb(pv)
                if not last:
                    conv_silu(nx, V1, q)
                t1_out(it, 2)
                if not last:
                    conv_taps(nx, K_)
                x_out(it, 2)
                if tail:
                    t_ms(pv, q)
                if not last:
                    conv_silu(nx, K_, q)
                t1_out(it, 3)
                if not last:
                    conv_taps(nx, Q_)
                    gates_of(nx, q)
                x_out(it, 3)
                z_silu(it, 0, p)
                if tail:
                    t_gate(pv, q)
                if not last:
                    conv_silu(nx, Q_, q)
                x_out4(it)
                z_silu(it, 1, p)
                if tail:
                    t_acc(pv)
                if not last:
                    products_out(nx)
                x_out5(it)

            nc.vector.memset(ones, 1.0)
            nc.vector.memset(zeros, 0.0)
            for z_ in (LTD, XT, T1F, X64, T15):
                nc.vector.memset(z_, 0.0)
            nc.vector.memset(expo[:, 0, :], 0.5)
            nc.vector.memset(expo[:, 1, :], -0.5)
            for i in range(2):
                a = nc.vector.memset(raw[i][:, :, 0:KCONV - 1], 0.0)
            a.then_inc(set_pool, 1)
            dve.wait_ge(in_misc, 48)
            tt(rowa, rowb[:, HV:2 * HV], rowb[:, 2 * HV:3 * HV], ALU.add).then_inc(set_dve, 1)
            dve.wait_ge(set_pool, 1)
            dve.wait_ge(in_wv, 32)
            for c in (V0, V1):
                conv_taps((0, 0), c)
            for c in (V0, V1):
                conv_silu((0, 0), c, 0)
            dve.wait_ge(set_dve, 1)
            dve.wait_ge(set_pe, 1)
            abv = SB[0].rearrange("p (t n) -> p t n", t=NT)

            def rows_of(r):
                return r.unsqueeze(1).to_broadcast([P, NT, HV])

            tt(gb, abv[:, :, 0:HV], rows_of(rowb[:, 0:HV]), ALU.add)
            tt(ga, abv[:, :, HV:2 * HV], rows_of(rowa), ALU.add).then_inc(set_pool, 1)
            dve.wait_ge(set_pool, 2)
            stt(gab, ga, -1.0, ga, ALU.mult, ALU.max).then_inc(set_dve, 1)
            ts(ga, ga, 0.0, None, ALU.max).then_inc(set_dve, 1)
            dve.wait_ge(in_wkq, 32)
            for c in (K_, Q_):
                conv_taps((0, 0), c)
            dve.wait_ge(set_act, 2)
            dve.wait_ge(set_dve, 3)
            tt(gl, gl, ga, ALU.add).then_inc(set_dve, 1)
            dve.wait_ge(set_dve, 4)
            stt(gg, gl, -1.0, rows_of(eal), ALU.mult, ALU.mult).then_inc(set_dve, 1)
            for c in (K_, Q_):
                conv_silu((0, 0), c, 0)
            dve.wait_ge(set_dve, 5)
            dve.wait_ge(set_act, 5)
            gf = gates.rearrange("p h (f t v) -> p h f t v", f=NF, v=2)
            for h in range(HK):
                hv = slice(2 * h, 2 * h + 2)
                nc.vector.tensor_copy(gf[:, h, F_G], gg[:, :, hv])
                ts(gf[:, h, F_BETA], gb[:, :, hv], 0.5, 0.5, ALU.mult, ALU.add)
                a = ts(gf[:, h, F_NEG], gf[:, h, F_EG], -1.0, None, ALU.mult)
            a.then_inc(set_dve, 1)
            dve.wait_ge(set_dve, 6)
            gates_of((0, 0), 0)
            wait(dve, scd, (0, 0), 1)
            dve.wait_ge(in_const, 16)
            products_out((0, 0))
            run_steps(dve, step)
            t_w1(LAST, 1)
            t_osb(LAST)
            t_ms(LAST, 1)
            t_gate(LAST, 1)
            t_acc(LAST)

        @block.gpsimd
        def _(pool):
            pt_ = nc.gpsimd.tensor_tensor

            def decay_rows(nx, p):
                wait(pool, scd, nx, 1)
                for g in range(2):
                    wait(pool, diff, nx, g + 1 - 2)
                    src = sc[p][:, F_G, 4 * g:4 * g + 4].rearrange("p (c v) -> p v c", v=2)
                    pt_(gm[:, g].rearrange("p (v c) t -> p v c t", v=2),
                        uinc.unsqueeze(1).unsqueeze(1).to_broadcast([P, 2, 2, P]),
                        src.unsqueeze(3).to_broadcast([P, 2, 2, P]), ALU.mult).then_inc(gmd.handle, 1)

            def t_root(pv):
                wait(pool, msd, pv, 1)
                pt_(rO, msb, expo[:, 1, :], ALU.pow).then_inc(rOd.handle, 1)

            def t_scale(pv):
                wait(pool, rOd, pv, 1)
                for g in range(2):
                    pt_(osc[:, g], osb[:, g], rO[:, 4 * g:4 * g + 4].unsqueeze(2).to_broadcast([P, 4, P]), ALU.mult).then_inc(oscd.handle, 1)

            def step(it, first, last):
                hk, pair = it
                p, q = pair % 2, 1 - pair % 2
                nx, pv = (hk, pair + 1), (hk, pair - 1)
                wait(pool, kssd, it, 1)
                pt_(irt[p], kss_h, expo[:, 0, 0:TPS], ALU.pow).then_inc(irtd.handle, 1)
                wait(pool, ltd, it, 1)
                pt_(LTD[:, 0], LT[:, 0], rep4(C_B32), ALU.mult).then_inc(ltdP.handle, 1)

                def expand(l):
                    wait(pool, xtpd, it, 2 * l + 1)
                    pt_(XT[:, 0].rearrange("p a (b t) -> p a b t", t=Q32), XTp[:, 0].unsqueeze(2).to_broadcast([P, 4, P // Q32, Q32]),
                        rep4(C_B32).rearrange("p a (b t) -> p a b t", t=Q32), ALU.mult).then_inc(xeP.handle, 1)

                expand(0)
                wait(pool, ltd, it, 2)
                for g in range(2):
                    pt_(LT4[:, g], LT[:, g], rep4(C_L32), ALU.mult).then_inc(lt4d.handle, 1)
                expand(1)
                for g in range(2):
                    wait(pool, exp_, it, g + 1)
                    kv = kkqm[:, g, :, 1, :].unsqueeze(1).to_broadcast([P, 2, 2, P])
                    pt_(PT[p][:, g].rearrange("p (v c) t -> p v c t", v=2), E[:, g].rearrange("p (v c) t -> p v c t", v=2), kv, ALU.mult).then_inc(ptd.handle, 1)
                expand(2)
                expand(3)
                if not first:
                    t_root(pv)
                    t_scale(pv)
                expand(4)
                if not last:
                    decay_rows(nx, q)

            pool.wait_ge(in_const, 16)
            pool.wait_ge(set_pool, 1)
            pool.wait_ge(in_misc, 48)
            pool.wait_ge(in_wo, 16)
            pt_(wo, wo, nw.unsqueeze(2).to_broadcast([P, HV, HID]), ALU.mult).then_inc(wo_scaled, 1)
            decay_rows((0, 0), 0)
            pool.wait_ge(in_acc, 16)
            pt_(acc, acc, rowb[:, 4 * HV:].unsqueeze(1).to_broadcast([P, NT, HID]), ALU.add).then_inc(acc_biased, 1)
            run_steps(pool, step)
            t_root(LAST)
            t_scale(LAST)


def experts(nc, cst, acc, gate_t, w_e, xs, ys, out):
    with ExitStack() as ctx:
        def sb(name, *shape, dt=F32, parts=P):
            return ctx.enter_context(nc.sbuf_tensor(name, [parts, *shape], dt))[:]

        def bank(name):
            return ctx.enter_context(nc.psum_tensor(name, [P, 512], F32))[:]

        def sem(name):
            return ctx.enter_context(nc.semaphore(name))

        def sig(name):
            return Sig(sem(name), 1, U)

        ident = cst[:, C_ID:C_ID + P]
        before = cst[:, C_KKQ:C_KKQ + P]
        stats, mv, veps, rstd = sb("stats", NT, 6), sb("mv", NT, 2), sb("veps", NT), sb("rstd", NT)
        half = sb("half", NT)
        gw = sb("gw", KC, NE)
        x1T = [sb(f"x1T{i}", KC, P) for i in range(2)]
        probs, picked = sb("probs", NT, NE), sb("picked", NT, NE)
        mx, rs = sb("mx", NT), sb("rs", NT)
        v8 = sb("v8", NT, TOPK)
        prior = sb("prior", NT + 1, NE)
        allones = sb("allones", P)
        cnt_i, tiles_i = sb("cnt_i", NE, dt=I32), sb("tiles_i", NE, dt=I32)
        tiles, cum, base, base1 = sb("tiles", NE), sb("cum", NE), sb("base", NE), sb("base1", NE)
        pos, p8 = sb("pos", NT, NE), sb("p8", NT, TOPK)
        idx = sb("idx", NT, TOPK, dt=I32)
        cmp_ = sb("cmp", 2, NE)
        ec = sb("ec", 2)
        eidf = sb("eidf", 1 + 2 * P, parts=1)
        newf, turnsf = sb("newf", 2 * P, parts=1), sb("turnsf", 2 * P, parts=1)
        eid, new = sb("eid", 2 * P, dt=I32, parts=1), sb("new", 2 * P, dt=I32, parts=1)
        shifted, packedf = sb("shifted", 2 * P // U, U, parts=1), sb("packedf", 2 * P // U, parts=1)
        packed = sb("packed", 2 * P // U, dt=I32, parts=1)
        onesrow = sb("onesrow", 2 * P, parts=1)
        nth, place = sb("nth", 2 * P, dt=I32, parts=1), sb("place", 2 * P, dt=I32, parts=1)
        eq = sb("eq", NT, NE)
        eqp = sb("eqp", NT, NE)
        wj = sb("wj", TOPK, NT)
        we = sb("we", U * WCOL)
        xr = [sb(f"xr{i}", HID) for i in range(U)]
        yr = [sb(f"yr{i}", HID) for i in range(U)]
        xeT = [sb(f"xeT{i}", KC * P) for i in range(2)]
        sg = [sb(f"sg{i}", P) for i in range(2)]
        hr, hT = [sb(f"hr{i}", P) for i in range(2)], [sb(f"hT{i}", P) for i in range(2)]
        gath = [sb(f"gath{i}", TOPK, HID) for i in range(2)]
        PS = [bank(f"ps{i}") for i in range(8)]
        RT, LB, PF = PS[0:2], PS[2:4], PS[4:6]
        CB, EB = PS[6], PS[7]

        in_gw, ln_stats, ln_var, ln_eps, ln_root, x1d = (sem(n) for n in ("in_gw", "ln_stats", "ln_var", "ln_eps", "ln_root", "x1d"))
        rt, rte, lg, mxd, sub, ex, sm, rsd, prd, v8d, repd, pick = (
            sem(n) for n in ("rt", "rte", "lg", "mxd", "sub", "ex", "sm", "rsd", "prd", "v8d", "repd", "pick"))
        prid, pfd, cntd, tl, cumd, bsd, posd, p8d, idxd, cmpd, ecd, ebd, eidd, scat, ones_d = (
            sem(n) for n in ("prid", "pfd", "cntd", "tl", "cumd", "bsd", "posd", "p8d", "idxd", "cmpd", "ecd", "ebd", "eidd", "scat", "ones_d"))

        eqd, wjd = sem("eqd"), sem("wjd")
        x_in, w_in, y_out_d = ([sem(f"{n}{u}") for u in range(U)] for n in ("x_in", "w_in", "y_st"))
        trd, xtd, gud, sgd, hd, thd, htd, w2d, yd = (sig(n) for n in ("trd", "xtd", "gud", "sgd", "hd", "thd", "htd", "w2d", "yd"))
        g_in = [sem(f"g_in{i}") for i in range(2)]
        summed, fin_stats, fin_var, fin_eps, fin_root, fin_x, out_sem = (sem(n) for n in ("summed", "fin_stats", "fin_var", "fin_eps", "fin_root", "fin_x", "out_sem"))

        with nc.Block() as block:
            @block.sync
            def _(sp):
                sp.dma_start(gw, gate_t).then_inc(in_gw, 16)

            @block.gpsimd
            def _(pool):
                for g in range(NT // LNG):
                    of = slice(g * LNG, (g + 1) * LNG)
                    pool.wait_ge(ln_eps, g + 1)
                    nc.gpsimd.tensor_tensor(rstd[:, of], veps[:, of], half[:, of], ALU.pow).then_inc(ln_root, 1)
                pool.wait_ge(idxd, 1)
                for t in range(NT):
                    for j in range(TOPK):
                        nc.gpsimd.indirect_dma_start(out=xs, out_offset=bass.IndirectOffsetOnAxis(idx[:, t, j:j + 1].bitcast(U32), 0),
                                                     in_=acc[:, t, :], in_offset=None).then_inc(scat, 16)
                pool.wait_ge(scat, 16 * NT * TOPK)

            @block.scalar
            def _(act):
                def exponentials(i):
                    act.wait_ge(sub, i + 1)
                    nc.scalar.activation(picked[:, HT * i:HT * (i + 1), :], probs[:, HT * i:HT * (i + 1), :], ACT.Exp).then_inc(ex, 1)

                for t in range(NT):
                    act.wait_ge(rt, t + 1)
                    if t >= 2:
                        act.wait_ge(lg, t - 1)
                    nc.scalar.activation(x1T[t % 2].rearrange("p k t -> p (k t)"), RT[t % 2][:, 0:KC * P], ACT.Copy).then_inc(rte, 1)
                    if t == NT * 3 // 4 - 1:
                        exponentials(0)
                exponentials(1)

            @block.tensor
            def _(pe):
                pe.wait_ge(in_gw, 16)

                def logits(t):
                    pe.wait_ge(rte, t + 1)
                    for k in range(KC):
                        m = nc.tensor.matmul(LB[t // 8][:, (t % 8) * NE:(t % 8 + 1) * NE], x1T[t % 2][:, k, :], gw[:, k, :], start=k == 0, stop=k == KC - 1)
                    m.then_inc(lg, 1)

                for t in range(NT):
                    pe.wait_ge(x1d, t + 1)
                    if t >= 2:
                        pe.wait_ge(rte, t - 1)
                    for k in range(KC):
                        m = nc.tensor.transpose(RT[t % 2][:, k * P:(k + 1) * P], acc[:, t, k * P:(k + 1) * P], ident)
                    m.then_inc(rt, 1)
                    if t:
                        logits(t - 1)
                logits(NT - 1)
                for i in range(2):
                    pe.wait_ge(pick, i + 1)
                    pe.wait_ge(prid, HT * (i + 1))
                    nc.tensor.matmul(PF[i], before, picked[:, 8 * i:8 * i + 8, :].rearrange("p t e -> p (t e)"), start=True, stop=False)
                    nc.tensor.matmul(PF[i], allones, prior[:, 8 * i:8 * i + 8, :].rearrange("p t e -> p (t e)"), start=False, stop=True).then_inc(pfd, 1)
                nc.tensor.matmul(CB[:, 0:NE], allones, prior[:, NT, :], start=True, stop=True).then_inc(cntd, 1)
                pe.wait_ge(ecd, 2)
                for i in range(2):
                    m = nc.tensor.transpose(EB[0:1, i * P:(i + 1) * P], ec[:, i:i + 1], ident)
                m.then_inc(ebd, 1)

            @block.vector
            def _(dve):
                tt, stt, ts = nc.vector.tensor_tensor, nc.vector.scalar_tensor_tensor, nc.vector.tensor_scalar
                nc.vector.memset(half, -0.5)
                nc.vector.memset(onesrow, 1.0)
                nc.vector.memset(prior[:, 0, :], 0.0)
                nc.vector.memset(allones, 1.0).then_inc(ones_d, 1)
                for g in range(NT // LNG):
                    tiles_of = range(g * LNG, (g + 1) * LNG)
                    for t in tiles_of:
                        nc.vector.bn_stats(stats[:, t, :], acc[:, t, :]).then_inc(ln_stats, 1)
                    for t in tiles_of:
                        dve.wait_ge(ln_stats, t + 1)
                        nc.vector.bn_aggr(mv[:, t, :], stats[:, t, :]).then_inc(ln_var, 1)
                    dve.wait_ge(ln_var, (g + 1) * LNG)
                    ts(veps[:, g * LNG:(g + 1) * LNG], mv[:, g * LNG:(g + 1) * LNG, 1], LN_EPS, None, ALU.add).then_inc(ln_eps, 1)
                for t in range(NT):
                    if t % LNG == 0:
                        dve.wait_ge(ln_root, t // LNG + 1)
                    ts(acc[:, t, :], acc[:, t, :], mv[:, t, 0:1], rstd[:, t:t + 1], ALU.subtract, ALU.mult).then_inc(x1d, 1)
                for i in range(2):
                    half_of = slice(HT * i, HT * (i + 1))
                    lv = LB[i].rearrange("p (t e) -> p t e", e=NE)
                    dve.wait_ge(lg, HT * (i + 1))
                    nc.vector.reduce_max(mx[:, half_of], lv, mybir.AxisListType.X).then_inc(mxd, 1)
                    dve.wait_ge(mxd, i + 1)
                    tt(probs[:, half_of, :], lv, mx[:, half_of].unsqueeze(2).to_broadcast([P, HT, NE]), ALU.subtract).then_inc(sub, 1)
                    dve.wait_ge(ex, i + 1)
                    nc.vector.reduce_sum(mx[:, half_of], picked[:, half_of, :], mybir.AxisListType.X).then_inc(sm, 1)
                    dve.wait_ge(sm, i + 1)
                    nc.vector.reciprocal(rs[:, half_of], mx[:, half_of]).then_inc(rsd, 1)
                    dve.wait_ge(rsd, i + 1)
                    tt(probs[:, half_of, :], picked[:, half_of, :], rs[:, half_of].unsqueeze(2).to_broadcast([P, HT, NE]), ALU.mult).then_inc(prd, 1)
                    dve.wait_ge(prd, i + 1)
                    for t in range(HT * i, HT * (i + 1)):
                        nc.vector.max(v8[:, t, :], probs[:, t, :]).then_inc(v8d, 1)
                    for t in range(HT * i, HT * (i + 1)):
                        dve.wait_ge(v8d, t + 1)
                        nc.vector.match_replace(eq[:, t, :], v8[:, t, :], probs[:, t, :], -1.0).then_inc(repd, 1)
                    dve.wait_ge(repd, HT * (i + 1))
                    ts(picked[:, half_of, :], eq[:, half_of, :], 0.0, None, ALU.is_lt).then_inc(pick, 1)
                    dve.wait_ge(pick, i + 1)
                    for t in range(HT * i, HT * (i + 1)):
                        if t:
                            dve.wait_ge(prid, t)
                        tt(prior[:, t + 1, :], prior[:, t, :], picked[:, t, :], ALU.add).then_inc(prid, 1)
                dve.wait_ge(cntd, 1)
                ts(cnt_i, CB[:, 0:NE], float(P - 1), None, ALU.add).then_inc(tl, 1)
                dve.wait_ge(tl, 1)
                ts(tiles_i, cnt_i, P.bit_length() - 1, None, ALU.logical_shift_right).then_inc(tl, 1)
                dve.wait_ge(tl, 2)
                nc.vector.tensor_copy(tiles, tiles_i).then_inc(tl, 1)
                dve.wait_ge(tl, 3)
                nc.vector.tensor_tensor_scan(cum, allones[:, 0:NE], tiles, 0.0, ALU.mult, ALU.add).then_inc(cumd, 1)
                dve.wait_ge(cumd, 1)
                tt(base, cum, tiles, ALU.subtract).then_inc(bsd, 1)
                tt(cmp_, cum.unsqueeze(1).to_broadcast([P, 2, NE]), cst[:, C_TAU:C_TAU + 2].unsqueeze(2).to_broadcast([P, 2, NE]), ALU.is_le).then_inc(cmpd, 1)
                dve.wait_ge(bsd, 1)
                ts(base1, base, float(P), 1.0, ALU.mult, ALU.add).then_inc(bsd, 1)
                dve.wait_ge(cmpd, 1)
                nc.vector.reduce_sum(ec, cmp_, mybir.AxisListType.X).then_inc(ecd, 1)
                dve.wait_ge(ecd, 1)
                ts(ec, ec, float(NE - 1), None, ALU.min).then_inc(ecd, 1)
                dve.wait_ge(pfd, 2)
                dve.wait_ge(bsd, 2)
                for i in range(2):
                    tt(pos[:, 8 * i:8 * i + 8, :], PF[i].rearrange("p (t e) -> p t e", e=NE), base1.unsqueeze(1).to_broadcast([P, 8, NE]), ALU.add).then_inc(posd, 1)
                dve.wait_ge(posd, 2)
                tt(pos, pos, picked, ALU.mult).then_inc(posd, 1)
                dve.wait_ge(posd, 3)
                for t in range(NT):
                    nc.vector.max(p8[:, t, :], pos[:, t, :]).then_inc(p8d, 1)
                dve.wait_ge(p8d, NT)
                ts(idx, p8, 1.0, None, ALU.subtract).then_inc(idxd, 1)
                dve.wait_ge(ebd, 1)
                nc.vector.memset(eidf[:, 0:1], -1.0)
                nc.vector.tensor_copy(eid, EB[0:1, 0:2 * P])
                nc.vector.tensor_copy(eidf[:, 1:], EB[0:1, 0:2 * P]).then_inc(eidd, 1)
                dve.wait_ge(eidd, 1)
                tt(newf, eidf[:, 1:], eidf[:, 0:2 * P], ALU.not_equal).then_inc(eidd, 1)
                dve.wait_ge(eidd, 2)
                nc.vector.tensor_copy(new, newf)
                nc.vector.tensor_tensor_scan(turnsf, onesrow, newf, 0.0, ALU.mult, ALU.add).then_inc(eidd, 1)
                dve.wait_ge(eidd, 3)
                ts(nth, turnsf, -1.0, None, ALU.add).then_inc(eidd, 1)
                dve.wait_ge(eidd, 4)
                ts(place, nth, U - 1, None, ALU.bitwise_and).then_inc(eidd, 1)
                dve.wait_ge(eidd, 5)
                tt(shifted, place.rearrange("p (n u) -> p n u", u=U), cst[0:1, C_U:C_U + U].unsqueeze(1).to_broadcast([1, 2 * P // U, U]), ALU.mult).then_inc(eidd, 1)
                dve.wait_ge(eidd, 6)
                nc.vector.reduce_sum(packedf, shifted, mybir.AxisListType.X).then_inc(eidd, 1)
                dve.wait_ge(eidd, 7)
                nc.vector.tensor_copy(packed, packedf).then_inc(eidd, 1)
                dve.wait_ge(eidd, 8)
                for j in range(TOPK):
                    if j:
                        dve.wait_ge(wjd, j)
                    tt(eq, pos, p8[:, :, j:j + 1].to_broadcast([P, NT, NE]), ALU.is_equal).then_inc(eqd, 1)
                    dve.wait_ge(eqd, 2 * j + 1)
                    tt(eqp, eq, probs, ALU.mult).then_inc(eqd, 1)
                    dve.wait_ge(eqd, 2 * j + 2)
                    nc.vector.reduce_sum(wj[:, j, :], eqp, mybir.AxisListType.X).then_inc(wjd, 1)

        with nc.Block() as block:
            def begun(turn, u, n):
                return not isinstance(turn, int) or turn > 0 or u >= n

            def to_come(turn, u, n):
                return not isinstance(turn, int) or turn * U + u + n < XT_TILES

            def run_turns(eng, step):
                for u in range(U):
                    step((0, u), first=u == 0, last=False)
                with eng.Fori(1, XTURNS - 1) as turn:
                    for u in range(U):
                        step((turn, u), first=False, last=False)
                for u in range(U):
                    step((XTURNS - 1, u), first=False, last=u == U - 1)

            @block.sync
            def _(sp):
                def step(it, first, last):
                    turn, u = it
                    tile = turn * U + u
                    wait(sp, w2d, (turn, u - U), 1)
                    begins = sp.value_load(new[0:1, bass.ds(tile, 1)], min_val=0, max_val=1)
                    with sp.If(begins > 0):
                        e = sp.value_load(eid[0:1, bass.ds(tile, 1)], min_val=0, max_val=NE - 1)
                        to = sp.value_load(place[0:1, bass.ds(tile, 1)], min_val=0, max_val=U - 1)
                        sp.dma_start(we[:, bass.ds(to * WCOL, WCOL)], w_e[bass.ds(e, 1)].rearrange("a p n -> p (a n)")).then_inc(w_in[u], 16)
                    with sp.Else():
                        sp.sem_inc(w_in[u], 16)

                run_turns(sp, step)

            @block.gpsimd
            def _(pool):
                def step(it, first, last):
                    turn, u = it
                    wait(pool, trd, (turn, u - U), 1)
                    pool.dma_start(xr[u], xs[bass.ds((turn * U + u) * P, P), :]).then_inc(x_in[u], 16)

                run_turns(pool, step)

            @block.tensor
            def _(pe):
                def turn_x(tile):
                    turn, u = tile
                    pe.wait_ge(x_in[u % U], (turn + u // U) * 16 + 16)
                    for k in range(KC):
                        m = nc.tensor.transpose(PS[u % 2][:, k * P:(k + 1) * P], xr[u % U][:, k * P:(k + 1) * P], ident)
                    m.then_inc(trd.handle, 1)

                def load_places(turn):
                    return pe.value_load(packed[0:1, bass.ds(turn, 1)], min_val=0, max_val=(1 << UBITS * U) - 1)

                def weights_of(places, u):
                    at = ((places >> (UBITS * u)) & (U - 1)) * WCOL
                    return [pe.snap(at + 2 * k * INTER) for k in range(KC + 1)]

                def turn_h(tile):
                    turn, u = tile
                    wait(pe, hd, tile, 1)
                    nc.tensor.transpose(PS[6 + u % 2][:, 0:P], hr[u % 2], ident).then_inc(thd.handle, 1)

                def down(tile, at):
                    turn, u = tile
                    wait(pe, htd, tile, 1)
                    wait(pe, yd, (turn, u - 2), 1)
                    nc.tensor.matmul(PS[4 + u % 2][:, 0:HID], hT[u % 2], we[:, bass.ds(at[KC], HID)], start=True, stop=True).then_inc(w2d.handle, 1)

                def step(it, first, last):
                    turn, u = it
                    if u == 0:
                        places["before"] = load_places(turn - 1) if begun(turn, u, 1) else None
                        places["this"] = load_places(turn)
                    at = places[u] = weights_of(places["this"], u)
                    pe.wait_ge(w_in[u], turn * 16 + 16)
                    wait(pe, xtd, it, 1)
                    for k in range(KC):
                        m = nc.tensor.matmul(PS[2 + u % 2][:, 0:2 * INTER], xeT[u % 2][:, k * P:(k + 1) * P],
                                             we[:, bass.ds(at[k], 2 * INTER)], start=k == 0, stop=k == KC - 1)
                    m.then_inc(gud.handle, 1)
                    if begun(turn, u, 1):
                        turn_h((turn, u - 1))
                    if to_come(turn, u, 2):
                        turn_x((turn, u + 2))
                    if begun(turn, u, 2):
                        down((turn, u - 2), places[u - 2] if u >= 2 else weights_of(places["before"], U + u - 2))

                places = {}
                turn_x((0, 0))
                turn_x((0, 1))
                run_turns(pe, step)
                turn_h((XTURNS - 1, U - 1))
                down((XTURNS - 1, U - 2), places[U - 2])
                down((XTURNS - 1, U - 1), places[U - 1])

            @block.scalar
            def _(act):
                def y_out(tile):
                    turn, u = tile
                    wait(act, w2d, tile, 1)
                    n = (turn + (u - U) // U) * 16 + 16
                    if not (isinstance(n, int) and n <= 0):
                        act.wait_ge(y_out_d[u % U], n)
                    nc.scalar.activation(yr[u % U], PS[4 + u % 2][:, 0:HID], ACT.Copy).then_inc(yd.handle, 1)
                    wait(act, yd, tile, 1)
                    act.dma_start(ys[bass.ds((turn * U + u) * P, P), :], yr[u % U]).then_inc(y_out_d[u % U], 16)

                def step(it, first, last):
                    turn, u = it
                    wait(act, gud, it, 1)
                    nc.scalar.activation(sg[u % 2], PS[2 + u % 2][:, 0:P], ACT.Silu).then_inc(sgd.handle, 1)
                    if begun(turn, u, 2):
                        y_out((turn, u - 2))

                run_turns(act, step)
                y_out((XTURNS - 1, U - 2))
                y_out((XTURNS - 1, U - 1))
                for u in range(U):
                    act.wait_ge(y_out_d[u], 16 * XTURNS)

            @block.vector
            def _(dve):
                def h_out(tile):
                    turn, u = tile
                    wait(dve, sgd, tile, 1)
                    nc.vector.tensor_tensor(hr[u % 2], sg[u % 2], PS[2 + u % 2][:, P:2 * P], ALU.mult).then_inc(hd.handle, 1)

                def ht_out(tile):
                    turn, u = tile
                    wait(dve, thd, tile, 1)
                    nc.vector.tensor_copy(hT[u % 2], PS[6 + u % 2][:, 0:P]).then_inc(htd.handle, 1)

                def x_out(tile):
                    turn, u = tile
                    wait(dve, trd, tile, 1)
                    nc.vector.tensor_copy(xeT[u % 2], PS[u % 2][:, 0:KC * P]).then_inc(xtd.handle, 1)

                def step(it, first, last):
                    turn, u = it
                    if not first:
                        ht_out((turn, u - 1))
                    h_out(it)
                    if to_come(turn, u, 2):
                        x_out((turn, u + 2))

                x_out((0, 0))
                x_out((0, 1))
                run_turns(dve, step)
                ht_out((XTURNS - 1, U - 1))

        with nc.Block() as block:
            @block.gpsimd
            def _(pool):
                def root(g):
                    of = slice(g * LNG, (g + 1) * LNG)
                    pool.wait_ge(fin_eps, g + 1)
                    nc.gpsimd.tensor_tensor(rstd[:, of], veps[:, of], half[:, of], ALU.pow).then_inc(fin_root, 1)

                for t in range(NT):
                    if t >= 2:
                        pool.wait_ge(summed, TOPK * (t - 1))
                    for j in range(TOPK):
                        nc.gpsimd.indirect_dma_start(out=gath[t % 2][:, j, :], out_offset=None, in_=ys,
                                                     in_offset=bass.IndirectOffsetOnAxis(idx[:, t, j:j + 1].bitcast(U32), 0)).then_inc(g_in[t % 2], 16)
                    if t % LNG == 1 and t > LNG:
                        root(t // LNG - 1)
                root(NT // LNG - 1)

            @block.vector
            def _(dve):
                ts = nc.vector.tensor_scalar

                def normed(g):
                    dve.wait_ge(fin_root, g + 1)
                    for t in range(g * LNG, (g + 1) * LNG):
                        ts(acc[:, t, :], acc[:, t, :], mv[:, t, 0:1], rstd[:, t:t + 1], ALU.subtract, ALU.mult).then_inc(fin_x, 1)

                for t in range(NT):
                    dve.wait_ge(g_in[t % 2], 16 * TOPK * (t // 2 + 1))
                    for j in range(TOPK):
                        if t or j:
                            dve.wait_ge(summed, TOPK * t + j)
                        nc.vector.scalar_tensor_tensor(acc[:, t, :], gath[t % 2][:, j, :], wj[:, j, t:t + 1], acc[:, t, :], ALU.mult, ALU.add).then_inc(summed, 1)
                    dve.wait_ge(summed, TOPK * (t + 1))
                    nc.vector.bn_stats(stats[:, t, :], acc[:, t, :]).then_inc(fin_stats, 1)
                    dve.wait_ge(fin_stats, t + 1)
                    nc.vector.bn_aggr(mv[:, t, :], stats[:, t, :]).then_inc(fin_var, 1)
                    if t % LNG == LNG - 1:
                        dve.wait_ge(fin_var, t + 1)
                        ts(veps[:, t + 1 - LNG:t + 1], mv[:, t + 1 - LNG:t + 1, 1], LN_EPS, None, ALU.add).then_inc(fin_eps, 1)
                    if t % LNG == 2 and t > LNG:
                        normed(t // LNG - 1)
                normed(NT // LNG - 1)

            @block.sync
            def _(sp):
                for t in range(NT):
                    sp.wait_ge(fin_x, t + 1)
                    sp.dma_start(out[t * P:(t + 1) * P, :], acc[:, t, :]).then_inc(out_sem, 16)
                sp.wait_ge(out_sem, 16 * NT)


def build(nc, x_t, x_n, w_v, w_kq, w_z, prm, w_ab, rows, w_out, norm_w, consts, gate_t, w_e, xs, ys, out):
    with ExitStack() as ctx:
        cst = ctx.enter_context(nc.sbuf_tensor("cst", [P, NCONST], F32))[:]
        acc = ctx.enter_context(nc.sbuf_tensor("acc", [P, NT, HID], F32))[:]
        with nc.sbuf_tensor("zeros", [P, ZROWS * HID], F32) as zeros:
            attention(nc, cst, acc, zeros[:], x_t, x_n, w_v, w_kq, w_z, prm, w_ab, rows, w_out, norm_w, consts, xs)
        experts(nc, cst, acc, gate_t, w_e, xs, ys, out)


OUT_NAMES = ["out_0_dram"]


def kernel(**inputs):
    import numpy as np
    import concourse.bacc as bacc
    from concourse.bass_utils import run_bass_kernel_spmd as run

    a = {k[len("L0_"):]: np.asarray(v) for k, v in inputs.items()}
    x = a["attn_hidden_states"].reshape(TOK, HID)

    def by_partition(w):
        return w.reshape(KC, P, -1).transpose(1, 0, 2)

    wq, wk, wvv = np.split(a["attn_Wqkv"], [HK * P, 2 * HK * P])

    def heads(w, n):
        return w.reshape(HK, n, HID).transpose(0, 2, 1).reshape(HK, KC, P, n).transpose(0, 2, 1, 3)

    per_channel = np.concatenate([a["attn_bqkv"][:, None], a["attn_conv_b"][:, None], a["attn_conv_w"]], 1)
    cq, ck, cv = (t.reshape(HK, -1, P, NPRM) for t in np.split(per_channel, [HK * P, 2 * HK * P]))
    prm = np.concatenate([np.concatenate([cv, ck, cq], 1).transpose(0, 2, 1, 3).reshape(HK, P, 4 * NPRM),
                          a["attn_bz"].reshape(HK, REP, P).transpose(0, 2, 1)], 2)
    row = np.concatenate([a["attn_bb"], a["attn_ba"], a["attn_dt_bias"], a["attn_A_log"], a["attn_bout"]])

    r, c = np.meshgrid(np.arange(P), np.arange(P), indexing="ij")

    def joins(n, r, c):
        return (r // (2 * n) == c // (2 * n)) & (r // n % 2 == 1) & (c // n % 2 == 0)

    parts = [r == c, r <= c, r > c, r < c, r <= c, r // Q32 == c // Q32, joins(Q32, c, r)]
    parts += [joins(1 << l, r % Q32, c % Q32)[:, :Q32] for l in range(PACKED + 1)]
    parts.append((r % Q32 == c % Q32)[:, :Q32])
    parts.append(np.stack([np.arange(P), P + np.arange(P)], 1))
    parts.append(np.broadcast_to(float(U) ** np.arange(U), (P, U)))
    masks = np.concatenate([np.asarray(m, np.float32) for m in parts], 1)
    w13 = a["ffn_w13"].reshape(NE, 2, INTER, KC, P).transpose(0, 4, 3, 1, 2).reshape(NE, P, 2 * KC * INTER)

    arrays = {
        "x_t": by_partition(x.T),
        "x_n": x.reshape(NT, P, HID).transpose(1, 0, 2),
        "w_v": heads(wvv, 2 * P),
        "w_kq": np.concatenate([heads(wk, P), heads(wq, P)], 3),
        "w_z": heads(a["attn_Wz"], 2 * P),
        "prm": prm,
        "w_ab": by_partition(np.concatenate([a["attn_Wb"], a["attn_Wa"]]).T),
        "rows": np.broadcast_to(row, (P, row.size)),
        "w_out": a["attn_Wout"].T.reshape(HV, P, HID).transpose(1, 0, 2),
        "norm_w": a["attn_norm_w"][:, None],
        "consts": masks,
        "gate_t": by_partition(a["ffn_gate_w"].T),
        "w_e": np.concatenate([w13, a["ffn_w2"].transpose(0, 2, 1)], 2),
    }
    arrays = {k: np.ascontiguousarray(v) for k, v in arrays.items()}
    nc = bacc.Bacc("TRN2", target_bir_lowering=False, num_devices=1)
    args = [nc.dram_tensor(k, v.shape, mybir.dt.from_np(v.dtype), kind="ExternalInput").ap() for k, v in arrays.items()]
    out = nc.dram_tensor("out_0_dram", (TOK, HID), F32, kind="ExternalOutput").ap()
    xs = nc.dram_tensor("pairs_in", (SLOTS, HID), F32).ap()
    ys = nc.dram_tensor("pairs_out", (SLOTS, HID), F32).ap()
    build(nc, *args, xs, ys, out)
    res = run(nc, [arrays], core_ids=[0])
    return res.results[0]["out_0_dram"].reshape(NB, SEQ, HID)
```
